# Optimizing a Trainium2 kernel written in Bass

```python
import numpy as np
import jax
import jax.numpy as jnp

def _softmax(x, axis=-1):
    return jax.nn.softmax(x, axis=axis)

def _gelu(x):
    return jax.nn.gelu(x, approximate=True)

def _silu(x):
    return jax.nn.silu(x)

def _sigmoid(x):
    return jax.nn.sigmoid(x)

def _layernorm(x, axis=-1, eps=1e-05):
    m = jnp.mean(x, axis=axis, keepdims=True)
    v = jnp.var(x, axis=axis, keepdims=True)
    return (x - m) / jnp.sqrt(v + eps)

def _scatter_add(tgt, idx, src, axis=0):
    return tgt.at[idx].add(src)

def _segment_sum(src, seg, n):
    return jax.ops.segment_sum(src, seg, n)
kernel_name = 'mk_adj_preln_d2_adj_r2_4a706d'

def setup_inputs(seed: int=0):
    np.random.seed(seed)
    _w = jnp.asarray

    def _rec_inputs():
        import jax
        import jax.numpy as jnp
        _gk = jax.random.key(seed)
        x = -0.0002928 + 1 * jax.random.normal(jax.random.fold_in(_gk, 1), (32, 256, 256), jnp.float32)
        _a = jax.random.bernoulli(jax.random.fold_in(_gk, 2), 0.015625, (32, 256, 256))
        _a = jnp.logical_or(_a, jnp.swapaxes(_a, -1, -2))
        _a = jnp.logical_or(_a, jnp.eye(256, dtype=bool))
        adj = _a.astype(jnp.int32)
        return (x, adj)
    x, adj = _rec_inputs()

    def _L0_gnn_setup():
        import jax, jax.numpy as jnp
        import numpy as np
        ALPHA = 0.2

        def _leaky(x):
            return jnp.where(x >= 0, x, ALPHA * x)
        key = jax.random.key(seed)
        k1, k2, k3, k4 = jax.random.split(key, 4)
        B, N, F_in, F_out = (4, 1024, 256, 256)
        h = jax.random.normal(k1, (B, N, F_in), dtype=jnp.float32)
        W = jax.random.normal(k2, (F_in, F_out), dtype=jnp.float32) * 0.05
        a = jax.random.normal(k3, (2 * F_out, 1), dtype=jnp.float32) * 0.05
        adj = jax.random.randint(k4, (B, N, N), 0, 2, dtype=jnp.int32)
        return {'h': h, 'W': W, 'a': a, 'adj': adj}
    _L0_gnn_all = _L0_gnn_setup()
    _L0_gnn_in = {k: v for k, v in _L0_gnn_all.items() if k in ('W', 'a')}
    del _L0_gnn_all

    def _L1_gnn_setup():
        import jax, jax.numpy as jnp
        import numpy as np
        B, N, H, NH = (8, 512, 256, 8)
        DK = H // NH
        key = jax.random.key(seed)
        ks = jax.random.split(key, 6)
        x = jax.random.normal(ks[0], (B, N, H), dtype=jnp.float32)
        adj = jax.random.randint(ks[1], (B, N, N), 0, 2, dtype=jnp.int32)
        adj = jnp.maximum(adj, jnp.eye(N, dtype=jnp.int32)[None])
        s = 1.0 / np.sqrt(H)
        Wq = jax.random.normal(ks[2], (H, H), dtype=jnp.float32) * s
        Wk = jax.random.normal(ks[3], (H, H), dtype=jnp.float32) * s
        Wv = jax.random.normal(ks[4], (H, H), dtype=jnp.float32) * s
        Wg = jax.random.normal(ks[5], (H, 2 * H), dtype=jnp.float32) * (1.0 / np.sqrt(2 * H))
        bg = jnp.zeros((H,), dtype=jnp.float32)
        return {'x': x, 'adj': adj, 'Wq': Wq, 'Wk': Wk, 'Wv': Wv, 'Wg': Wg, 'bg': bg}
    _L1_gnn_all = _L1_gnn_setup()
    _L1_gnn_in = {k: v for k, v in _L1_gnn_all.items() if k in ('Wq', 'Wk', 'Wv', 'Wg', 'bg')}
    del _L1_gnn_all
    return {'x': x, 'adj': adj, 'L0_gnn_W': _L0_gnn_in['W'], 'L0_gnn_a': _L0_gnn_in['a'], 'L1_gnn_Wq': _L1_gnn_in['Wq'], 'L1_gnn_Wk': _L1_gnn_in['Wk'], 'L1_gnn_Wv': _L1_gnn_in['Wv'], 'L1_gnn_Wg': _L1_gnn_in['Wg'], 'L1_gnn_bg': _L1_gnn_in['bg']}

def reference(x, adj, L0_gnn_W, L0_gnn_a, L1_gnn_Wq, L1_gnn_Wk, L1_gnn_Wv, L1_gnn_Wg, L1_gnn_bg):
    import jax
    import jax.numpy as jnp

    def _L0_gnn_ref(h, W, a, adj):
        import jax, jax.numpy as jnp
        import numpy as np
        ALPHA = 0.2

        def _leaky(x):
            return jnp.where(x >= 0, x, ALPHA * x)
        F_out = W.shape[1]
        Wh = jnp.matmul(h, W)
        Wh_sg = jax.lax.stop_gradient(Wh)
        a1 = a[:F_out, 0]
        a2 = a[F_out:, 0]
        s_i = Wh_sg @ a1
        s_j = Wh_sg @ a2
        e = _leaky(s_i[:, :, None] + s_j[:, None, :])
        e = jnp.where(adj > 0, e, jnp.float32(-9000000000000000.0))
        attention = jax.nn.softmax(e, axis=1)
        h_prime = jnp.einsum('bij,bjf->bif', attention, Wh)
        return _leaky(h_prime)

    def _L1_gnn_ref(x, adj, Wq, Wk, Wv, Wg, bg):
        import jax, jax.numpy as jnp
        import numpy as np
        B, N, H, NH = (8, 512, 256, 8)
        DK = H // NH
        b, n, h = x.shape
        q = (x @ Wq.T).reshape(b, n, NH, DK)
        k = (x @ Wk.T).reshape(b, n, NH, DK)
        v = (x @ Wv.T).reshape(b, n, NH, DK)
        scores = jnp.einsum('bqhd,bkhd->bhqk', q, k) / jnp.sqrt(jnp.float32(DK))
        mask = (adj != 0)[:, None, :, :]
        scores = jnp.where(mask, scores, -jnp.inf)
        attn = jax.nn.softmax(scores, axis=-1)
        c = jnp.einsum('bhqk,bkhd->bqhd', attn, v).reshape(b, n, h)
        gate = jax.nn.sigmoid(jnp.concatenate([c, x], axis=2) @ Wg.T + bg)
        return gate * x + (1.0 - gate) * c
    h = jnp.maximum(_layernorm(x, axis=-1), 0.0)
    x = x + _L0_gnn_ref(h, L0_gnn_W, L0_gnn_a, adj)
    h = jnp.maximum(_layernorm(x, axis=-1), 0.0)
    x = x + _L1_gnn_ref(h, adj, L1_gnn_Wq, L1_gnn_Wk, L1_gnn_Wv, L1_gnn_Wg, L1_gnn_bg)
    return x

_drawn_inputs = setup_inputs


def setup_inputs(seed=0):
    import zlib

    import numpy as np

    out = dict(_drawn_inputs(seed))
    spreads = {'L1_gnn_bg': (0.0, 0.539)}
    factors = {}
    for name, (base, spread) in spreads.items():
        noise = np.random.default_rng([zlib.crc32(name.encode()), seed]).standard_normal(out[name].shape)
        drawn = base * np.exp(spread * noise) if base else spread * noise
        out[name] = jnp.asarray(drawn.astype(out[name].dtype))
    for name, factor in factors.items():
        out[name] = (out[name] * factor).astype(out[name].dtype)
    return out
```

```python
import concourse.bass as bass
from concourse import mybir
from contextlib import ExitStack


def gnn_kernel(nc: bass.Bass, x, adj, w0, a0, wq, wk, wv, wg, bg, out):
    f32, f32r, bf16, i32 = mybir.dt.float32, mybir.dt.float32r, mybir.dt.bfloat16, mybir.dt.int32
    ALU = mybir.AluOpType
    ACT = mybir.ActivationFunctionType

    B, N, F = x.shape
    P = 128
    NH = 8
    DK = F // NH
    PAIRS = B // 2
    T = 2 * N // P
    NT = 2 * N
    FT = F // P
    HG = P // DK
    UN = 2 * NH
    NEG = -1e30
    BIG = 3e38
    SLOPE = 0.2
    EPS = 1e-5
    EMAX = 1e18
    SCALE = float(DK) ** -0.5
    KR = 3 * DK
    KM = KR + 2
    PTS = 6

    x_v = x.rearrange("(n a) (i p) c -> n p (a i) c", a=2, p=P)
    adj_v = adj.rearrange("(n a) (i p) c -> n p (a i) c", a=2, p=P)
    out_v = out.rearrange("(n a) (i p) c -> n p (a i) c", a=2, p=P)

    ctx = ExitStack()
    with ctx:
        def sb(name, shape, dt):
            return ctx.enter_context(nc.sbuf_tensor(name, shape, dt))

        def sem(name):
            return ctx.enter_context(nc.semaphore(name))

        def sems(name, n):
            return [sem(f"{name}{k}") for k in range(n)]

        ident = sb("ident", [P, P], f32)
        identb = sb("identb", [P, P], bf16)
        ones = sb("ones", [P, DK], f32)
        w0h, w0l = sb("w0h", [P, FT, F + 2], f32r), sb("w0l", [P, FT, F + 2], f32r)
        wqh, wql = sb("wqh", [P, FT, F], f32r), sb("wql", [P, FT, F], f32r)
        wkh, wkl = sb("wkh", [P, FT, F], f32r), sb("wkl", [P, FT, F], f32r)
        wvh, wvl = sb("wvh", [P, FT, F], f32r), sb("wvl", [P, FT, F], f32r)
        wgh, wgl = sb("wgh", [P, 2 * FT, F], f32r), sb("wgl", [P, 2 * FT, F], f32r)
        nbg = sb("nbg", [P, FT], f32)
        eps = sb("eps", [P, 1], f32)
        tiny_d, tiny_p = sb("tiny_d", [1, 64], f32), sb("tiny_p", [1, 64], f32)
        X = sb("X", [P, T, F], f32)
        ADJ = sb("ADJ", [P, T, N], i32)
        CL = sb("CL", [P, T, N], bf16)
        M0 = sb("M0", [P, T, N], bf16)
        M1 = [sb(f"M1_{k}", [P, T, N], bf16) for k in range(2)]
        MN = [sb(f"MN_{k}", [P, T, N], bf16) for k in range(2)]
        XN = sb("XN", [P, T, F], f32)
        HTh, HTl = sb("HTh", [P, FT, NT], f32r), sb("HTl", [P, FT, NT], f32r)
        WH = sb("WH", [P, T, F + 2], f32)
        E0 = sb("E0", [P, T, N], f32)
        X1 = [sb(f"X1_{k}", [P, T, F], f32) for k in range(2)]
        H2h = [sb(f"H2h_{k}", [P, FT, NT], f32r) for k in range(2)]
        H2l = [sb(f"H2l_{k}", [P, FT, NT], f32r) for k in range(2)]
        PRh = [sb(f"PRh_{k}", [P, NT], f32r) for k in range(2)]
        PRl = [sb(f"PRl_{k}", [P, NT], f32r) for k in range(2)]
        QS = [sb(f"QS_{k}", [P, NH, NT], f32r) for k in range(2)]
        KS = [sb(f"KS_{k}", [P, NH, NT], f32r) for k in range(2)]
        V = [sb(f"V_{k}", [P, T, F], f32) for k in range(2)]
        bst = sb("bst", [P, T, 6], f32)
        mv = sb("mv", [P, T, 2], f32)
        rstd = sb("rstd", [P, T], f32)
        mx0 = sb("mx0", [P, T], f32)
        nm0 = sb("nm0", [P, T], f32)
        ngm = sb("ngm", [P, T], f32)
        rs0 = sb("rs0", [P, T], f32)
        ri0 = sb("ri0", [P, T], f32)
        NM = sb("NM", [P, T, NH], f32)
        MH, ML = sb("MH", [NH, N], f32r), sb("ML", [NH, N], f32r)
        PT = [sb(f"PT{k}", [P, 2 * N], f32) for k in range(PTS)]
        RI = sb("RI", [P, FT, N], f32)
        C = sb("C", [P, FT, NT], f32)
        Ch, Cl = sb("Ch", [P, FT, NT], f32r), sb("Cl", [P, FT, NT], f32r)
        D = sb("D", [P, FT, NT], f32)
        G = sb("G", [P, FT, NT], f32)

        def bank(name):
            return ctx.enter_context(nc.psum_tensor(name, [P, 512], f32))

        G0, G1, S0, S1, T0, T1, BC, BR = [bank(n) for n in ("G0", "G1", "S0", "S1", "T0", "T1", "BC", "BR")]
        SB, TB = [S0, S1], [T0, T1]

        c_made, w_in, a_in, wa_made, w_tr, w_hi, w_lo, ks_ones, bg_neg = [
            sem(n) for n in ("c_made", "w_in", "a_in", "wa_made", "w_tr", "w_hi", "w_lo", "ks_ones", "bg_neg")]
        x_in, adj_in, out_done = sem("x_in"), sem("adj_in"), sem("out_done")
        stacked = sems("stacked", 4)
        max_in = sems("max_in", 2)
        ln_bst, ln_mv, ln_log, ln_rstd, ln_xn = [sems(n, 2) for n in ("ln_bst", "ln_mv", "ln_log", "ln_rstd", "ln_xn")]
        h_t, h_hi, h_lo = sems("h_t", 4), sems("h_hi", 4), sems("h_lo", 4)
        adj_cut, mn_made, adj_t, clt_made, m0_made, m1_made = [
            sem(n) for n in ("adj_cut", "mn_made", "adj_t", "clt_made", "m0_made", "m1_made")]
        wh_mm, wh_out, sib_t, e0_max, e0_nm, e0_ngm, e0_add, e0_leaky, e0_exp, e0_rinv, wh_norm = [
            sem(n) for n in ("wh_mm", "wh_out", "sib_t", "e0_max", "e0_nm", "e0_ngm", "e0_add", "e0_leaky", "e0_exp", "e0_rinv", "wh_norm")]
        hp_mm, hp_relu, hp_x, x1_made = [sem(n) for n in ("hp_mm", "hp_relu", "hp_x", "x1_made")]
        qk_mm, qk_hi, qk_lo = sem("qk_mm"), sem("qk_hi"), sem("qk_lo")
        v_mm, v_out = sem("v_mm"), sem("v_out")
        s_mm, s_max = sems("s_mm", 4), sems("s_max", 4)
        m_t, m_hi, m_lo = sem("m_t"), sem("m_hi"), sem("m_lo")
        st_mm, p_exp = sems("st_mm", 4), sems("p_exp", 4)
        pv_mm = sem("pv_mm")
        r_log, r_inv, c_made_, c_hi, c_lo, d_sub, d_made = [
            sem(n) for n in ("r_log", "r_inv", "c_out", "c_hi", "c_lo", "d_sub", "d_made")]
        z_mm, z_exp = sem("z_mm"), sem("z_exp")
        g_cut, g_log, g_made, gd_made, r_made = [sem(n) for n in ("g_cut", "g_log", "g_made", "gd_made", "r_made")]
        r_t, fin = sem("r_t"), sem("fin")

        def count(pair, k=1, per=1):
            base, off = pair
            c = off * per + k
            if base is None:
                return c if off >= 0 else None
            return (base if per == 1 else base * per) + c if c else (base if per == 1 else base * per)

        def after(eng, s, pair, k=1, per=1):
            value = count(pair, k, per)
            if value is not None:
                eng.wait_ge(s, value)

        slot = [0]

        def after_apart(eng, *waits):
            for w in waits:
                after(eng, *w)
            if waits[0][1][0] is not None:
                slot[0] = (slot[0] + 1) % 64
                at = slice(slot[0], slot[0] + 1)
                if eng is nc.vector:
                    eng.memset(tiny_d[:, at], 0.0)
                else:
                    eng.tensor_tensor(tiny_p[:, at], ones[0:1, 0:1], ones[0:1, 1:2], ALU.add)

        def of_unit(s, pair, u):
            return s[u % 4], pair, u // 4 + 1, 4

        def unit(eng, s, pair, u):
            after(eng, *of_unit(s, pair, u))

        def pipeline(eng, body):
            for n in (0, 1):
                body((None, n), n % 2, n >= 0, n >= 1, n >= 2, True)
            with eng.Fori(2, PAIRS - 2, 2) as i:
                for d in (0, 1):
                    body((i, d), d, True, True, True, True)
            for n in range(PAIRS - 2, PAIRS + 2):
                body((None, n), n % 2, n < PAIRS, n <= PAIRS, True, n + 1 < PAIRS)

        def prev(pair, n=1):
            return pair[0], pair[1] - n

        def pair_index(pair):
            base, off = pair
            return off if base is None else base + off if off else base

        block = ctx.enter_context(nc.Block())

        @block.sync
        def _(sp):
            stage = {"wq": XN[:, 0:2, :], "wk": XN[:, 2:4, :], "wv": E0[:, 0:2, :]}
            sp.dma_start(X[:, :, :], x_v[0]).then_inc(x_in, 16)
            sp.dma_start(ADJ[:, :, :], adj_v[0]).then_inc(adj_in, 16)
            sp.dma_start(WH[:, 0:2, 0:F], w0.rearrange("(f p) o -> p f o", p=P)).then_inc(a_in, 16)
            sp.dma_start(E0[:, 2:4, :], a0.rearrange("(j o) u -> u j o", j=2).broadcast_to([P, 2, F])).then_inc(a_in, 16)
            for name, w in (("wq", wq), ("wk", wk), ("wv", wv)):
                sp.dma_start(stage[name], w.rearrange("(f p) c -> p f c", p=P)).then_inc(w_in, 16)
            sp.dma_start(G[:, :, :], wg.rearrange("(f p) c -> p f c", p=P)).then_inc(w_in, 16)
            with nc.allow_non_contiguous_dma(reason="256 numbers, once"):
                sp.dma_start(rstd[:, 0:2], bg.rearrange("(f p) -> p f", p=P)).then_inc(a_in, 16)

            def stack(u, pair, par):
                o, dst = u // 2, (QS, KS)[u % 2][par]
                rows = ((0, 0), (0, 1), (1, 2)) if u % 2 == 0 else ((0, 0), (1, 1), (0, 2))
                for lo, j in rows:
                    after(sp, qk_lo if lo else qk_hi, pair, u + 1, 4)
                    src = (PRl if lo else PRh)[u % 2]
                    for g in range(HG):
                        sp.dma_start(dst[j * DK:(j + 1) * DK, o * HG + g, :].bitcast(f32),
                                     src[g * DK:(g + 1) * DK, :].bitcast(f32)).then_inc(stacked[u], 16)

            def maximum_rows(a, pair, par):
                after(sp, m_hi, pair, a + 1, 2)
                sp.dma_start(QS[par][KR:KR + 1, :, a * N:(a + 1) * N].bitcast(f32), MH[:, :].bitcast(f32)).then_inc(max_in[a], 16)
                after(sp, m_lo, pair, a + 1, 2)
                sp.dma_start(QS[par][KR + 1:KR + 2, :, a * N:(a + 1) * N].bitcast(f32), ML[:, :].bitcast(f32)).then_inc(max_in[a], 16)

            def body(i, par, A, Bs, Cs, more):
                b, c = prev(i), prev(i, 2)
                if A and more:
                    after(sp, adj_cut, i)
                    after(sp, mn_made, i)
                    sp.dma_start(ADJ[:, :, :], adj_v[pair_index(prev(i, -1))]).then_inc(adj_in, 16)
                if Bs:
                    maximum_rows(0, b, 1 - par)
                if Cs:
                    for h in range(2):
                        after(sp, fin, c, h + 1, 2)
                        sp.dma_start(out_v[pair_index(c)][:, 2 * h:2 * h + 2, :],
                                     X1[par][:, 2 * h:2 * h + 2, :]).then_inc(out_done, 16)
                if A and more:
                    after(sp, hp_x, i, 2, 2)
                    sp.dma_start(X[:, :, :], x_v[pair_index(prev(i, -1))]).then_inc(x_in, 16)
                if A:
                    stack(0, i, par)
                    stack(1, i, par)
                if Bs:
                    maximum_rows(1, b, 1 - par)
                if A:
                    stack(2, i, par)
                    stack(3, i, par)

            pipeline(sp, body)
            sp.wait_ge(out_done, 2 * 16 * PAIRS)

        @block.gpsimd
        def _(pool):
            pool.memset(ident[:, :], 0.0).then_inc(c_made, 1)
            pool.memset(identb[:, :], 0.0).then_inc(c_made, 1)
            pool.memset(ones[:, :], 1.0).then_inc(c_made, 1)
            pool.memset(eps[:, :], EPS).then_inc(c_made, 1)
            pool.wait_ge(c_made, 4)
            for m in (ident, identb):
                pool.affine_select(out=m[:, :], in_=m[:, :], compare_op=ALU.not_equal, fill=1.0, base=0,
                                   pattern=[[-1, P]], channel_multiplier=1).then_inc(c_made, 1)
            pool.wait_ge(w_tr, 5)

            def normalise(k, src, pair):
                after_apart(pool, (ln_rstd[k], pair), (h_t[1], pair) if k else (h_t[3], prev(pair)))
                for t in range(T):
                    last = pool.tensor_scalar(XN[:, t, :], src[:, t, :], mv[:, t, 0:1], rstd[:, t:t + 1],
                                              ALU.subtract, ALU.mult)
                last.then_inc(ln_xn[k], 1)

            def split_c(a, pair, par):
                s = slice(a * N, (a + 1) * N)
                after(pool, c_hi, pair, a + 1, 2)
                pool.tensor_tensor(Cl[:, :, s], C[:, :, s], Ch[:, :, s].bitcast(f32), ALU.subtract).then_inc(c_lo, 1)
                if a == 0:
                    after(pool, r_t, prev(pair), 2, 2)
                pool.tensor_tensor(D[:, :, s], H2h[par][:, :, s].bitcast(f32), C[:, :, s], ALU.subtract).then_inc(d_sub, 1)
                after(pool, d_sub, pair, a + 1, 2)
                pool.tensor_tensor(D[:, :, s], D[:, :, s], H2l[par][:, :, s].bitcast(f32), ALU.add).then_inc(d_made, 1)

            def body(i, par, A, Bs, Cs, more):
                b, c = prev(i), prev(i, 2)
                if A:
                    after_apart(pool, (adj_in, i, 16, 16), (adj_t, b))
                    pool.tensor_scalar(CL[:, :, :], ADJ[:, :, :], 1.0, -1.0, ALU.min, ALU.max).then_inc(adj_cut, 1)
                    after_apart(pool, *(of_unit(s_max, c, u) for u in range(UN - 4, UN)))
                    pool.tensor_scalar(MN[par][:, :, :], ADJ[:, :, :], 0.0, NEG, ALU.is_equal, ALU.mult).then_inc(mn_made, 1)
                    normalise(0, X, i)
                    after_apart(pool, (clt_made, i))
                    pool.tensor_scalar(M0[:, :, :], M1[par][:, :, :], 0.0, NEG, ALU.is_le, ALU.mult).then_inc(m0_made, 1)
                if Cs:
                    split_c(1, c, par)
                if A:
                    after_apart(pool, (e0_max, i))
                    for t in range(T):
                        last = pool.tensor_scalar(E0[:, t, :], E0[:, t, :], WH[:, t, F + 1:F + 2], None, ALU.add)
                    last.then_inc(e0_add, 1)
                    pool.tensor_scalar(M1[par][:, :, :], M1[par][:, :, :], 0.0, NEG, ALU.is_equal, ALU.mult).then_inc(m1_made, 1)
                    after_apart(pool, (e0_rinv, i))
                    for t in range(T):
                        last = pool.tensor_scalar(WH[:, t, 0:F], WH[:, t, 0:F], ri0[:, t:t + 1], None, ALU.mult)
                    last.then_inc(wh_norm, 1)
                if Cs:
                    after(pool, d_made, c, 2, 2)
                    after(pool, g_made, c)
                    pool.tensor_tensor(D[:, :, :], D[:, :, :], G[:, :, :], ALU.mult).then_inc(gd_made, 1)
                if A:
                    after(pool, x_in, i, 16, 16)
                    for h in range(2):
                        after(pool, hp_relu, i, h + 1, 2)
                        s = X1[par][:, 2 * h:2 * h + 2, :]
                        pool.tensor_tensor(s, s, X[:, 2 * h:2 * h + 2, :], ALU.add).then_inc(hp_x, 1)
                    normalise(1, X1[par], i)
                if Bs:
                    split_c(0, b, 1 - par)

            pipeline(pool, body)

        @block.scalar
        def _(act):
            act.wait_ge(c_made, 6)
            srcs = [(S0, wqh), (S1, wkh), (T0, wvh)]
            for n, (ps, dst) in enumerate(srcs):
                act.wait_ge(w_tr, n + 1)
                act.activation(dst[:, :, :].rearrange("p f o -> p (f o)"), ps[:, :], ACT.Copy).then_inc(w_hi, 1)
            for n, ps in enumerate((BC, BR)):
                act.wait_ge(w_tr, 4 + n)
                act.activation(wgh[:, 2 * n:2 * n + 2, :].rearrange("p f o -> p (f o)"), ps[:, :], ACT.Copy).then_inc(w_hi, 1)
            act.wait_ge(wa_made, 4)
            act.activation(w0h[:, :, :], WH[:, 0:2, :], ACT.Copy).then_inc(w_hi, 1)
            act.wait_ge(bg_neg, 1)

            def inv_std(k, pair):
                after(act, ln_mv[k], pair)
                act.activation(rstd[:, :], mv[:, :, 1], ACT.Ln, bias=eps[:, 0:1]).then_inc(ln_log[k], 1)
                after(act, ln_log[k], pair)
                act.activation(rstd[:, :], rstd[:, :], ACT.Exp, scale=-0.5).then_inc(ln_rstd[k], 1)

            def relu_hi(layer, pair, dst, banks):
                for f in range(FT):
                    after(act, h_t[2 * layer + f], pair)
                    act.activation(dst[:, f, :], banks[f][:, :], ACT.Relu).then_inc(h_hi[2 * layer + f], 1)

            def exps(u, pair):
                unit(act, st_mm, pair, u)
                if u >= PTS:
                    after(act, pv_mm, pair, (u - PTS) // 4 + 1, 4)
                else:
                    after(act, pv_mm, prev(pair), (max(w for w in range(UN) if w % PTS == u)) // 4 + 1, 4)
                act.activation(PT[u % PTS][:, :], TB[u % 2][:, :], ACT.Exp, scale=SCALE).then_inc(p_exp[u % 4], 1)

            def inv_sum(a, pair):
                after(act, pv_mm, pair, 2 * a + 2, 4)
                after(act, c_made_, pair if a else prev(pair), 1 if a else 2, 2)
                act.activation(RI[:, :, :].rearrange("p f n -> p (f n)"), BR[:, :], ACT.Ln).then_inc(r_log, 1)
                after(act, r_log, pair, a + 1, 2)
                act.activation(RI[:, :, :], RI[:, :, :], ACT.Exp, scale=-1.0).then_inc(r_inv, 1)

            def c_high(a, pair):
                after(act, c_made_, pair, a + 1, 2)
                act.activation(Ch[:, :, a * N:(a + 1) * N], C[:, :, a * N:(a + 1) * N], ACT.Copy).then_inc(c_hi, 1)

            def body(i, par, A, Bs, Cs, more):
                b, c = prev(i), prev(i, 2)
                if Cs:
                    for u in range(NH, NH + 4):
                        exps(u, c)
                if A:
                    inv_std(0, i)
                if Cs:
                    for u in range(NH + 4, UN):
                        exps(u, c)
                if A:
                    relu_hi(0, i, HTh, (G0, G1))
                if Cs:
                    inv_sum(1, c)
                    c_high(1, c)
                if A:
                    for t in range(T):
                        after(act, wh_mm, i, t + 1, 4)
                        act.activation(WH[:, t, :], (G0, G1)[t % 2][:, 0:F + 2], ACT.Copy).then_inc(wh_out, 1)
                if Cs:
                    for o in range(FT):
                        after(act, z_mm, c, o + 1, 2)
                        act.activation(G[:, o, :], (BC, BR)[o][:, :], ACT.Exp, bias=nbg[:, o:o + 1], scale=-1.0).then_inc(z_exp, 1)
                if Bs:
                    exps(0, b)
                    exps(1, b)
                if A:
                    after(act, e0_leaky, i)
                    for t in range(T):
                        last = act.activation(E0[:, t, :], E0[:, t, :], ACT.Exp, bias=ngm[:, t:t + 1], accum_out=rs0[:, t:t + 1])
                    last.then_inc(e0_exp, 1)
                if Bs:
                    exps(2, b)
                if Cs:
                    after(act, g_cut, c)
                    act.activation(G[:, :, :], G[:, :, :], ACT.Ln).then_inc(g_log, 1)
                if Bs:
                    exps(3, b)
                if Cs:
                    after(act, g_log, c)
                    act.activation(G[:, :, :], G[:, :, :], ACT.Exp, scale=-1.0).then_inc(g_made, 1)
                if A:
                    if Bs:
                        exps(4, b)
                    after(act, out_done, c, 32, 32)
                    for h in range(2):
                        after(act, hp_mm, i, h + 1, 2)
                        act.activation(X1[par][:, 2 * h:2 * h + 2, :].rearrange("p t f -> p (t f)"), (G1, G0)[h][:, :], ACT.Relu,
                                       scale=1.0 - SLOPE).then_inc(hp_relu, 1)
                    if Bs:
                        for u in range(5, NH):
                            exps(u, b)
                    inv_std(1, i)
                elif Bs:
                    for u in range(4, NH):
                        exps(u, b)
                if Bs:
                    inv_sum(0, b)
                    c_high(0, b)
                if A:
                    relu_hi(1, i, H2h[par], (G1, G0))
                    for n, kind in enumerate((0, 1, "v", "v", 2, 3)):
                        ps = (G0, G1)[n % 2]
                        if kind == "v":
                            after(act, v_mm, i, n - 1, 2)
                            act.activation(V[par][:, 2 * n - 4:2 * n - 2, :].rearrange("p t f -> p (t f)"), ps[:, :], ACT.Copy).then_inc(v_out, 1)
                        else:
                            after(act, qk_mm, i, kind + 1, 4)
                            after(act, stacked[(kind + 2) % 4], i if kind >= 2 else b, 192, 192)
                            act.activation(PRh[kind % 2][:, :], ps[:, :], ACT.Copy).then_inc(qk_hi, 1)

            pipeline(act, body)

        @block.vector
        def _(dve):
            for k in range(2):
                last = dve.memset(KS[k][KR:KM, :, :].bitcast(f32), 1.0)
            last.then_inc(ks_ones, 1)
            dve.wait_ge(a_in, 48)
            for j in range(2):
                for f in range(FT):
                    dve.tensor_tensor_reduce(out=C[:, j, f * F:(f + 1) * F], in0=WH[:, f, 0:F], in1=E0[:, 2 + j, :], scale=1.0, scalar=0.0,
                                             op0=ALU.mult, op1=ALU.add, accum_out=WH[:, f, F + j:F + j + 1]).then_inc(wa_made, 1)
            dve.tensor_scalar(nbg[:, :], rstd[:, 0:2], -1.0, None, ALU.mult).then_inc(bg_neg, 1)
            for n, (ps, hi, lo) in enumerate(((S0, wqh, wql), (S1, wkh, wkl), (T0, wvh, wvl))):
                dve.wait_ge(w_hi, n + 1)
                dve.tensor_tensor(lo[:, :, :].rearrange("p f o -> p (f o)"), ps[:, :],
                                  hi[:, :, :].rearrange("p f o -> p (f o)").bitcast(f32), ALU.subtract).then_inc(w_lo, 1)
            for n, ps in enumerate((BC, BR)):
                dve.wait_ge(w_hi, 4 + n)
                dve.tensor_tensor(wgl[:, 2 * n:2 * n + 2, :].rearrange("p f o -> p (f o)"), ps[:, :],
                                  wgh[:, 2 * n:2 * n + 2, :].rearrange("p f o -> p (f o)").bitcast(f32), ALU.subtract).then_inc(w_lo, 1)
            dve.wait_ge(w_hi, 6)
            dve.wait_ge(wa_made, 4)
            dve.tensor_tensor(w0l[:, :, :], WH[:, 0:2, :], w0h[:, :, :].bitcast(f32), ALU.subtract).then_inc(w_lo, 1)
            dve.wait_ge(bg_neg, 1)

            def stats(k, src, pair):
                for t in range(T):
                    last = dve.bn_stats(bst[:, t, :], src[:, t, :])
                last.then_inc(ln_bst[k], 1)
                after_apart(dve, (ln_bst[k], pair), (ln_xn[1 - k], pair if k else prev(pair)))
                for t in range(T):
                    last = dve.bn_aggr(mv[:, t, :], bst[:, t, :])
                last.then_inc(ln_mv[k], 1)

            def relu_lo(layer, pair, dst, hi, banks):
                for f in range(FT):
                    after(dve, h_hi[2 * layer + f], pair)
                    dve.scalar_tensor_tensor(out=dst[:, f, :], in0=banks[f][:, :], scalar=0.0, in1=hi[:, f, :].bitcast(f32),
                                             op0=ALU.max, op1=ALU.subtract).then_inc(h_lo[2 * layer + f], 1)

            def score_max(u, pair, par):
                a, h = u // NH, u % NH
                if u == 0:
                    after_apart(dve, of_unit(s_mm, pair, u), (m_t, prev(pair), 2, 2))
                else:
                    after_apart(dve, of_unit(s_mm, pair, u))
                for t in range(2):
                    ps = SB[u % 2][:, t * N:(t + 1) * N]
                    last = dve.tensor_tensor_reduce(out=ps, in0=ps, in1=MN[par][:, 2 * a + t, :],
                                                    scale=-1.0, scalar=BIG, op0=ALU.add, op1=ALU.min,
                                                    accum_out=NM[:, 2 * a + t, h:h + 1])
                last.then_inc(s_max[u % 4], 1)

            def max_parts(a, pair, ps):
                after(dve, m_t, pair, a + 1, 2)
                after(dve, max_in[1 - a], pair if a else prev(pair), 32, 32)
                dve.tensor_copy(MH[:, :], ps[0:NH, 0:N]).then_inc(m_hi, 1)
                after(dve, m_hi, pair, a + 1, 2)
                dve.tensor_tensor(ML[:, :], ps[0:NH, 0:N], MH[:, :].bitcast(f32), ALU.subtract).then_inc(m_lo, 1)

            def attention_out(a, pair):
                after(dve, r_inv, pair, a + 1, 2)
                after(dve, z_mm, prev(pair), 2, 2)
                if a == 0:
                    after(dve, r_made, prev(pair))
                    after(dve, c_lo, prev(pair), 2, 2)
                dve.tensor_tensor(C[:, :, a * N:(a + 1) * N], BC[:, :].rearrange("p (f n) -> p f n", f=FT), RI[:, :, :],
                                  ALU.mult).then_inc(c_made_, 1)

            def body(i, par, A, Bs, Cs, more):
                b, c = prev(i), prev(i, 2)
                if A:
                    after(dve, x_in, i, 16, 16)
                    stats(0, X, i)
                if Bs:
                    after(dve, mn_made, b)
                    for u in range(0, NH):
                        score_max(u, b, 1 - par)
                if A:
                    relu_lo(0, i, HTl, HTh, (G0, G1))
                    after(dve, adj_t, i)
                    dve.tensor_copy(M1[par][:, :, :].rearrange("p t n -> p (t n)"), G0[:, :].bitcast(bf16)).then_inc(clt_made, 1)
                if Cs:
                    attention_out(1, c)
                if Bs:
                    max_parts(0, b, G1)
                if A:
                    after_apart(dve, (sib_t, i), (m0_made, i))
                    for t in range(T):
                        a = t // 2
                        last = dve.tensor_tensor_reduce(out=E0[:, t, :], in0=G0[:, a * N:(a + 1) * N], in1=M0[:, t, :], scale=1.0,
                                                        scalar=-BIG, op0=ALU.add, op1=ALU.max, accum_out=mx0[:, t:t + 1])
                    last.then_inc(e0_max, 1)
                    after(dve, e0_max, i)
                    dve.scalar_tensor_tensor(out=nm0[:, :], in0=mx0[:, :], scalar=-1.0, in1=WH[:, :, F + 1], op0=ALU.mult,
                                             op1=ALU.subtract).then_inc(e0_nm, 1)
                    after(dve, e0_nm, i)
                    dve.scalar_tensor_tensor(out=ngm[:, :], in0=nm0[:, :], scalar=SLOPE, in1=nm0[:, :], op0=ALU.mult,
                                             op1=ALU.min).then_inc(e0_ngm, 1)
                    after(dve, e0_ngm, i)
                    after(dve, e0_add, i)
                    e0 = E0[:, :, :].rearrange("p t n -> p (t n)")
                    dve.scalar_tensor_tensor(out=e0, in0=e0, scalar=SLOPE, in1=e0, op0=ALU.mult, op1=ALU.max).then_inc(e0_leaky, 1)
                if Cs:
                    after(dve, z_exp, c, 2, 2)
                    dve.tensor_scalar(G[:, :, :], G[:, :, :], EMAX, 1.0, ALU.min, ALU.add).then_inc(g_cut, 1)
                if Bs:
                    for u in (NH, NH + 1, NH + 2):
                        score_max(u, b, 1 - par)
                if A:
                    after(dve, e0_exp, i)
                    dve.reciprocal(ri0[:, :], rs0[:, :]).then_inc(e0_rinv, 1)
                if Bs:
                    score_max(NH + 3, b, 1 - par)
                if Cs:
                    after(dve, gd_made, c)
                    dve.tensor_tensor(D[:, :, :], D[:, :, :], C[:, :, :], ALU.add).then_inc(r_made, 1)
                    for h in range(2):
                        after(dve, r_t, c, h + 1, 2)
                        s = X1[par][:, 2 * h:2 * h + 2, :].rearrange("p t f -> p (t f)")
                        dve.tensor_tensor(s, (G1, G0)[h][:, :], s, ALU.add).then_inc(fin, 1)
                if A:
                    for h in range(2):
                        after(dve, hp_x, i, h + 1, 2)
                        s = X1[par][:, 2 * h:2 * h + 2, :].rearrange("p t f -> p (t f)")
                        dve.scalar_tensor_tensor(out=s, in0=(G1, G0)[h][:, :], scalar=SLOPE, in1=s, op0=ALU.mult,
                                                 op1=ALU.add).then_inc(x1_made, 1)
                    after(dve, x1_made, i, 2, 2)
                    stats(1, X1[par], i)
                if Bs:
                    for u in range(NH + 4, UN):
                        score_max(u, b, 1 - par)
                    attention_out(0, b)
                if A:
                    relu_lo(1, i, H2l[par], H2h[par], (G1, G0))
                if Bs:
                    max_parts(1, b, G1)
                if A:
                    for u in range(4):
                        after(dve, qk_hi, i, u + 1, 4)
                        after(dve, stacked[(u + 2) % 4], i if u >= 2 else b, 192, 192)
                        dve.tensor_tensor(PRl[u % 2][:, :], (G0, G1)[u % 2][:, :], PRh[u % 2][:, :].bitcast(f32),
                                          ALU.subtract).then_inc(qk_lo, 1)

            pipeline(dve, body)

        @block.tensor
        def _(pe):
            pe.wait_ge(c_made, 6)
            srcs = ((16, S0, XN[:, 0:2, :]), (32, S1, XN[:, 2:4, :]), (48, T0, E0[:, 0:2, :]),
                    (64, BC, G[:, :, 0:F]), (64, BR, G[:, :, F:2 * F]))
            pe.wait_ge(w_in, 64)
            for _, ps, src in srcs:
                for f in range(FT):
                    for o in range(FT):
                        last = pe.transpose(ps[:, f * F + o * P:f * F + (o + 1) * P], src[:, o, f * P:(f + 1) * P], ident[:, :])
                last.then_inc(w_tr, 1)
            pe.wait_ge(w_lo, 6)
            pe.wait_ge(ks_ones, 1)

            def split(ps, lh, ll, rh, rl, first, end):
                pe.matmul(ps, lh, rh, start=first, stop=False)
                pe.matmul(ps, lh, rl, start=False, stop=False)
                return pe.matmul(ps, ll, rh, start=False, stop=end)

            def feature_transposes(layer, banks):
                for f in range(FT):
                    for t in range(T):
                        last = pe.transpose(banks[f][:, t * P:(t + 1) * P], XN[:, t, f * P:(f + 1) * P], ident[:, :])
                    last.then_inc(h_t[2 * layer + f], 1)

            def scores(u, pair, par):
                a, h = u // NH, u % NH
                if u == 0:
                    for s in (0, 1):
                        after(pe, stacked[s], pair, 192, 192)
                if u == NH // 2:
                    for s in (2, 3):
                        after(pe, stacked[s], pair, 192, 192)
                if u >= 2:
                    unit(pe, s_max, pair, u - 2)
                else:
                    unit(pe, s_max, prev(pair), UN + u - 2)
                for t in range(2):
                    last = pe.matmul(SB[u % 2][:, t * N:(t + 1) * N], QS[par][0:KR, h, a * N + t * P:a * N + (t + 1) * P],
                                     KS[par][0:KR, h, a * N:(a + 1) * N], start=True, stop=True)
                last.then_inc(s_mm[u % 4], 1)

            def scores_t(u, pair, par):
                a, h = u // NH, u % NH
                if h == 0:
                    after(pe, max_in[a], pair, 32, 32)
                    after(pe, m1_made, pair)
                if u >= 2:
                    unit(pe, p_exp, pair, u - 2)
                else:
                    unit(pe, p_exp, prev(pair), UN + u - 2)
                ps = TB[u % 2]
                pe.matmul(ps[:, :], identb[:, :], M1[par][:, 2 * a:2 * a + 2, :].rearrange("p t n -> p (t n)"),
                          start=True, stop=False)
                for t in range(2):
                    last = pe.matmul(ps[:, t * N:(t + 1) * N], KS[par][0:KM, h, a * N + t * P:a * N + (t + 1) * P],
                                     QS[par][0:KM, h, a * N:(a + 1) * N], start=False, stop=(t == 1))
                last.then_inc(st_mm[u % 4], 1)

            def weighted(g, pair, par):
                a, o = g // 2, g % 2
                if o == 0:
                    if a == 0:
                        after(pe, z_exp, prev(pair), 2, 2)
                    else:
                        after(pe, c_made_, pair, 1, 2)
                for rhs_ones in (False, True):
                    ps = BR if rhs_ones else BC
                    for t in range(2):
                        for k in range(HG):
                            u = 4 * g + k
                            if t == 0 and not rhs_ones:
                                unit(pe, p_exp, pair, u)
                            lhs = ones[:, :] if rhs_ones else V[par][:, 2 * a + t, o * P + k * DK:o * P + (k + 1) * DK]
                            last = pe.matmul(ps[k * DK:(k + 1) * DK, o * N:(o + 1) * N], lhs, PT[u % PTS][:, t * N:(t + 1) * N],
                                             start=(t == 0), stop=(t == 1))
                last.then_inc(pv_mm, 1)

            def max_transposes(a, pair, ps):
                for u in range(NH * a + 4, NH * a + NH):
                    unit(pe, s_max, pair, u)
                for t in range(2):
                    last = pe.transpose(ps[0:NH, t * P:(t + 1) * P], NM[:, 2 * a + t, :], ident[:, :])
                last.then_inc(m_t, 1)

            def body(i, par, A, Bs, Cs, more):
                b, c = prev(i), prev(i, 2)
                for n in range(NH + 2):
                    if Cs and n < NH:
                        scores_t(NH + n, c, par)
                    if Bs and n >= 2:
                        scores(n - 2, b, 1 - par)
                    if Cs and n == 5:
                        after(pe, v_out, c, 2, 2)
                        weighted(2, c, par)
                if A:
                    after(pe, ln_xn[0], i)
                    after(pe, qk_lo, b, 4, 4)
                    feature_transposes(0, (G0, G1))
                if Cs:
                    weighted(3, c, par)
                if A:
                    after(pe, adj_cut, i)
                    after(pe, h_lo[0], i)
                    for t in range(T):
                        for j in range(2):
                            slot = ((t // 2) * 2 + j) * N + (t % 2) * P
                            last = pe.transpose(G0[:, :].bitcast(bf16)[:, slot:slot + P], CL[:, t, j * P:(j + 1) * P], identb[:, :])
                    last.then_inc(adj_t, 1)
                    after(pe, h_lo[1], i)
                if Bs:
                    if not A:
                        after(pe, qk_lo, b, 4, 4)
                    max_transposes(0, b, G1)
                if A:
                    after(pe, clt_made, i)
                    for t in range(T):
                        if t == 1 and Bs:
                            after(pe, m_lo, b, 1, 2)
                        if t >= 2:
                            after(pe, wh_out, i, t - 1, 4)
                        for f in range(FT):
                            last = split((G0, G1)[t % 2][:, 0:F + 2], HTh[:, f, t * P:(t + 1) * P], HTl[:, f, t * P:(t + 1) * P],
                                         w0h[:, f, :], w0l[:, f, :], f == 0, f == FT - 1)
                        last.then_inc(wh_mm, 1)
                    for t in range(T):
                        after(pe, wh_out, i, max(t + 1, 3), 4)
                        last = pe.transpose(G0[:, t * P:(t + 1) * P], WH[:, t, F:F + 1].broadcast_to([P, P]), ident[:, :])
                    last.then_inc(sib_t, 1)
                if Cs:
                    after(pe, c_made_, c, 2, 2)
                    def gate(o, half):
                        hi, lo = (H2h[par], H2l[par]) if half == "x" else (Ch, Cl)
                        for f in range(FT):
                            k = f + (FT if half == "x" else 0)
                            last = split((BC, BR)[o][:, :], wgh[:, k, o * P:(o + 1) * P], wgl[:, k, o * P:(o + 1) * P],
                                         hi[:, f, :], lo[:, f, :], half == "x" and f == 0, half == "c" and f == FT - 1)
                        return last
                    gate(0, "x")
                    gate(1, "x")
                    after(pe, c_lo, c, 2, 2)
                    gate(0, "c").then_inc(z_mm, 1)
                    gate(1, "c").then_inc(z_mm, 1)
                if Bs:
                    for n in range(4):
                        scores_t(n, b, 1 - par)
                        scores(NH + n, b, 1 - par)
                    after(pe, v_out, b, 2, 2)
                    weighted(0, b, 1 - par)
                if Cs:
                    after(pe, r_made, c)
                    if A:
                        after(pe, wh_out, i, 4, 4)
                    elif Bs:
                        after(pe, m_lo, b, 1, 2)
                    for h in range(2):
                        if h == 1 and A:
                            after(pe, e0_max, i)
                        for t in (2 * h, 2 * h + 1):
                            for f in range(FT):
                                last = pe.transpose((G1, G0)[h][:, (t % 2) * F + f * P:(t % 2) * F + (f + 1) * P],
                                                    D[:, f, t * P:(t + 1) * P], ident[:, :])
                        last.then_inc(r_t, 1)
                if A:
                    after(pe, wh_norm, i)
                    for a in range(2):
                        after(pe, fin, c, a + 1, 2)
                        for t in range(2):
                            for j in range(2):
                                last = pe.matmul((G1, G0)[a][:, t * F:(t + 1) * F], E0[:, 2 * a + j, t * P:(t + 1) * P],
                                                 WH[:, 2 * a + j, 0:F], start=(j == 0), stop=(j == 1))
                        last.then_inc(hp_mm, 1)
                if Bs:
                    for n in range(4, NH):
                        scores_t(n, b, 1 - par)
                        scores(NH + n, b, 1 - par)
                    weighted(1, b, 1 - par)
                if A:
                    after(pe, ln_xn[1], i)
                    after(pe, x1_made, i, 2, 2)
                    feature_transposes(1, (G1, G0))
                    after(pe, h_lo[2], i)
                if Bs:
                    if not A:
                        after(pe, fin, c, 1, 2)
                    max_transposes(1, b, G1)
                if A:
                    after(pe, h_lo[3], i)
                    for n, kind in enumerate((0, 1, "v", "v", 2, 3)):
                        ps = (G0, G1)[n % 2]
                        if kind == 1 and Bs:
                            after(pe, m_lo, b, 2, 2)
                        if n in (2, 3):
                            after(pe, qk_lo, i, n - 1, 4)
                        if n in (4, 5):
                            after(pe, v_out, i, n - 3, 2)
                        if kind == "v":
                            for t in (2 * n - 4, 2 * n - 3):
                                for f in range(FT):
                                    last = split(ps[:, (t % 2) * F:(t % 2 + 1) * F], H2h[par][:, f, t * P:(t + 1) * P],
                                                 H2l[par][:, f, t * P:(t + 1) * P], wvh[:, f, :], wvl[:, f, :], f == 0, f == FT - 1)
                            last.then_inc(v_mm, 1)
                        else:
                            o = kind // 2
                            wh_, wl_ = ((wqh, wql), (wkh, wkl))[kind % 2]
                            for f in range(FT):
                                last = split(ps[:, :], wh_[:, f, o * P:(o + 1) * P], wl_[:, f, o * P:(o + 1) * P],
                                             H2h[par][:, f, :], H2l[par][:, f, :], f == 0, f == FT - 1)
                            last.then_inc(qk_mm, 1)

            pipeline(pe, body)


_INS = ["x", "adj", "L0_gnn_W", "L0_gnn_a", "L1_gnn_Wq", "L1_gnn_Wk", "L1_gnn_Wv", "L1_gnn_Wg", "L1_gnn_bg"]


def kernel(**inputs):
    import numpy as _np
    import concourse.bacc as _bacc
    from concourse import mybir as _mybir
    from concourse.bass_utils import run_bass_kernel_spmd as _run

    nc = _bacc.Bacc("TRN2", target_bir_lowering=False, num_devices=1)
    arrays, args = {}, []
    for name in _INS:
        a = _np.ascontiguousarray(inputs[name])
        arrays[f"in_{name}"] = a
        args.append(nc.dram_tensor(f"in_{name}", a.shape, _mybir.dt.from_np(a.dtype), kind="ExternalInput").ap())
    shape = inputs["x"].shape
    args.append(nc.dram_tensor("out_dram", shape, _mybir.dt.from_np(_np.dtype("float32")), kind="ExternalOutput").ap())
    gnn_kernel(nc, *args)
    r = _run(nc, [arrays], core_ids=[0])
    return r.results[0]["out_dram"]
```

```python
import concourse.bass as bass
from concourse import mybir
from contextlib import ExitStack


def gnn_kernel(nc: bass.Bass, x, adj, w0, a0, wq, wk, wv, wg, bg, out):
    f32, f32r, bf16, i32 = mybir.dt.float32, mybir.dt.float32r, mybir.dt.bfloat16, mybir.dt.int32
    ALU = mybir.AluOpType
    ACT = mybir.ActivationFunctionType

    B, N, F = x.shape
    P = 128
    NH = 8
    DK = F // NH
    PAIRS = B // 2
    T = 2 * N // P
    NT = 2 * N
    FT = F // P
    HG = P // DK
    UN = 2 * NH
    NEG = -1e30
    BIG = 3e38
    SLOPE = 0.2
    EPS = 1e-5
    EMAX = 1e18
    SCALE = float(DK) ** -0.5
    KR = 3 * DK
    KM = KR + 2
    FIRST = 3
    PTS = 6

    x_v = x.rearrange("(n a) (i p) c -> n p (a i) c", a=2, p=P)
    adj_v = adj.rearrange("(n a) (i p) c -> n p (a i) c", a=2, p=P)
    out_v = out.rearrange("(n a) (i p) c -> n p (a i) c", a=2, p=P)

    ctx = ExitStack()
    with ctx:
        def sb(name, shape, dt):
            return ctx.enter_context(nc.sbuf_tensor(name, shape, dt))

        def sem(name):
            return ctx.enter_context(nc.semaphore(name))

        def sems(name, n):
            return [sem(f"{name}{k}") for k in range(n)]

        ident = sb("ident", [P, P], f32)
        identb = sb("identb", [P, P], bf16)
        ones = sb("ones", [P, DK], f32)
        w0h, w0l = sb("w0h", [P, FT, F + 2], f32r), sb("w0l", [P, FT, F + 2], f32r)
        wqh, wql = sb("wqh", [P, FT, F], f32r), sb("wql", [P, FT, F], f32r)
        wkh, wkl = sb("wkh", [P, FT, F], f32r), sb("wkl", [P, FT, F], f32r)
        wvh, wvl = sb("wvh", [P, FT, F], f32r), sb("wvl", [P, FT, F], f32r)
        wgh, wgl = sb("wgh", [P, 2 * FT, F], f32r), sb("wgl", [P, 2 * FT, F], f32r)
        nbg = sb("nbg", [P, FT], f32)
        eps = sb("eps", [P, 1], f32)
        tiny = sb("tiny", [1, 64], f32)
        X = sb("X", [P, T, F], f32)
        ADJ = sb("ADJ", [P, T, N], i32)
        CL = sb("CL", [P, T, N], bf16)
        M0 = sb("M0", [P, T, N], bf16)
        M1 = [sb(f"M1_{k}", [P, T, N], bf16) for k in range(2)]
        MN = [sb(f"MN_{k}", [P, T, N], bf16) for k in range(2)]
        XN = sb("XN", [P, T, F], f32)
        HTh, HTl = sb("HTh", [P, FT, NT], f32r), sb("HTl", [P, FT, NT], f32r)
        WH = sb("WH", [P, T, F + 2], f32)
        E0 = sb("E0", [P, T, N], f32)
        OUT = sb("OUT", [P, T, F], f32)
        X1 = [sb(f"X1_{k}", [P, T, F], f32) for k in range(2)]
        H2h = [sb(f"H2h_{k}", [P, FT, NT], f32r) for k in range(2)]
        H2l = [sb(f"H2l_{k}", [P, FT, NT], f32r) for k in range(2)]
        PRQl = sb("PRQl", [P, FT, NT], f32)
        QS = [sb(f"QS_{k}", [P, NH, NT], f32r) for k in range(2)]
        KS = [sb(f"KS_{k}", [P, NH, NT], f32r) for k in range(2)]
        V = [sb(f"V_{k}", [P, T, F], f32) for k in range(2)]
        bst = sb("bst", [P, T, 6], f32)
        mv = sb("mv", [P, T, 2], f32)
        rstd = sb("rstd", [P, T], f32)
        mx0 = sb("mx0", [P, T], f32)
        nm0 = sb("nm0", [P, T], f32)
        ngm = sb("ngm", [P, T], f32)
        rs0 = sb("rs0", [P, T], f32)
        ri0 = sb("ri0", [P, T], f32)
        NM = sb("NM", [P, T, NH], f32)
        MH, ML = sb("MH", [NH, N], f32r), sb("ML", [NH, N], f32r)
        PT = [sb(f"PT{k}", [P, 2 * N], f32) for k in range(PTS)]
        RI = sb("RI", [P, FT, N], f32)
        C = sb("C", [P, FT, NT], f32)
        Ch, Cl = sb("Ch", [P, FT, NT], f32r), sb("Cl", [P, FT, NT], f32r)
        D = sb("D", [P, FT, NT], f32)
        G = sb("G", [P, FT, NT], f32)
        PR = [[WH[:, :, :].rearrange("p t f -> p (t f)")[:, 0:FT * NT].rearrange("p (f n) -> p f n", f=FT), PRQl[:, :, :]],
              [E0[:, :, :].rearrange("p (f t) n -> p f (t n)", f=FT), G[:, :, :]]]

        def bank(name):
            return ctx.enter_context(nc.psum_tensor(name, [P, 512], f32))

        G0, G1, S0, S1, T0, T1, BC, BR = [bank(n) for n in ("G0", "G1", "S0", "S1", "T0", "T1", "BC", "BR")]
        SB, TB = [S0, S1], [T0, T1]

        c_made, w_in, a_in, wa_made, w_tr, w_hi, w_lo, ks_ones, bg_neg = [
            sem(n) for n in ("c_made", "w_in", "a_in", "wa_made", "w_tr", "w_hi", "w_lo", "ks_ones", "bg_neg")]
        x_in, adj_in, out_done = sem("x_in"), sem("adj_in"), sem("out_done")
        stacked = sems("stacked", 2)
        max_in = sems("max_in", 2)
        ln_bst, ln_mv, ln_log, ln_rstd, ln_xn = [sems(n, 2) for n in ("ln_bst", "ln_mv", "ln_log", "ln_rstd", "ln_xn")]
        h_t, h_hi, h_lo = sems("h_t", 4), sems("h_hi", 4), sems("h_lo", 4)
        xn_sub = sem("xn_sub")
        adj_cut, mn_made, adj_t, clt_made, m0_made, m1_made = [
            sem(n) for n in ("adj_cut", "mn_made", "adj_t", "clt_made", "m0_made", "m1_made")]
        wh_mm, wh_out, sib_t, e0_max, e0_nm, e0_ngm, e0_add, e0_leaky, e0_exp, e0_rinv, wh_norm = [
            sem(n) for n in ("wh_mm", "wh_out", "sib_t", "e0_max", "e0_nm", "e0_ngm", "e0_add", "e0_leaky", "e0_exp", "e0_rinv", "wh_norm")]
        hp_mm, hp_relu, hp_x, x1_made = [sem(n) for n in ("hp_mm", "hp_relu", "hp_x", "x1_made")]
        qk_mm, qk_hi, qk_lo = sem("qk_mm"), sem("qk_hi"), sem("qk_lo")
        v_mm, v_out = sem("v_mm"), sem("v_out")
        s_mm, s_max = sems("s_mm", 4), sems("s_max", 4)
        m_t, m_hi, m_lo = sem("m_t"), sem("m_hi"), sem("m_lo")
        st_mm, p_exp = sems("st_mm", 4), sems("p_exp", 4)
        pv_mm = sem("pv_mm")
        r_log, r_inv, c_out, c_hi, c_lo, d_sub, d_made = [
            sem(n) for n in ("r_log", "r_inv", "c_out", "c_hi", "c_lo", "d_sub", "d_made")]
        z_mm, z_exp = sem("z_mm"), sem("z_exp")
        g_cut, g_log, g_made, gd_made, r_made = [sem(n) for n in ("g_cut", "g_log", "g_made", "gd_made", "r_made")]
        r_t, fin = sem("r_t"), sem("fin")

        def count(pair, k=1, per=1):
            base, off = pair
            c = off * per + k
            if base is None:
                return c if off >= 0 else 0
            rows = base if per == 1 else base * per
            return rows + c if c else rows

        def of_unit(pair, u):
            return count(pair, u // 4 + 1, 4)

        held = [0]

        def hold(dve, pair):
            if pair[0] is not None:
                held[0] = (held[0] + 1) % 64
                dve.memset(tiny[:, held[0]:held[0] + 1], 0.0)

        def pipeline(eng, body):
            for n in range(FIRST):
                body((None, n), n % 2, n >= 0, n >= 1, n >= 2, True)
            with eng.Fori(FIRST, PAIRS - 2, 2) as i:
                for d in (0, 1):
                    body((i, d), (FIRST + d) % 2, True, True, True, True)
            for n in range(PAIRS - 1, PAIRS + 2):
                body((None, n), n % 2, n < PAIRS, n <= PAIRS, True, n + 1 < PAIRS)

        def prev(pair, n=1):
            return pair[0], pair[1] - n

        def pair_index(pair):
            base, off = pair
            return off if base is None else base + off if off else base

        block = ctx.enter_context(nc.Block())

        @block.sync
        def _(sp):
            stage = {"wq": XN[:, 0:2, :], "wk": XN[:, 2:4, :], "wv": E0[:, 0:2, :]}
            sp.dma_start(X[:, :, :], x_v[0]).then_inc(x_in, 16)
            sp.dma_start(ADJ[:, :, :], adj_v[0]).then_inc(adj_in, 16)
            sp.dma_start(WH[:, 0:2, 0:F], w0.rearrange("(f p) o -> p f o", p=P)).then_inc(a_in, 16)
            sp.dma_start(E0[:, 2:4, :], a0.rearrange("(j o) u -> u j o", j=2).broadcast_to([P, 2, F])).then_inc(a_in, 16)
            for name, w in (("wq", wq), ("wk", wk), ("wv", wv)):
                sp.dma_start(stage[name], w.rearrange("(f p) c -> p f c", p=P)).then_inc(w_in, 16)
            sp.dma_start(G[:, :, :], wg.rearrange("(f p) c -> p f c", p=P)).then_inc(w_in, 16)
            with nc.allow_non_contiguous_dma(reason="256 numbers, once"):
                sp.dma_start(rstd[:, 0:2], bg.rearrange("(f p) -> p f", p=P)).then_inc(a_in, 16)

            def stack(n, pair, par):
                dst, rows = ((QS, (0, 0, 1)), (KS, (0, 1, 0)))[n]
                for part in (0, 1):
                    sp.wait_ge((qk_hi, qk_lo)[part], count(pair, 2 * n + 2, 4))
                    for j in range(3):
                        if rows[j] == part:
                            for g in range(HG):
                                sp.dma_start(dst[par][j * DK:(j + 1) * DK, g:NH:HG, :].bitcast(f32),
                                             PR[n][part][g * DK:(g + 1) * DK, :, :]).then_inc(stacked[n], 16)

            def maximum_rows(a, pair, par):
                sp.wait_ge(m_hi, count(pair, a + 1, 2))
                sp.dma_start(QS[par][KR:KR + 1, :, a * N:(a + 1) * N].bitcast(f32), MH[:, :].bitcast(f32)).then_inc(max_in[a], 16)
                sp.wait_ge(m_lo, count(pair, a + 1, 2))
                sp.dma_start(QS[par][KR + 1:KR + 2, :, a * N:(a + 1) * N].bitcast(f32), ML[:, :].bitcast(f32)).then_inc(max_in[a], 16)

            def body(i, par, A, Bs, Cs, more):
                b, c = prev(i), prev(i, 2)
                if A and more:
                    sp.wait_ge(adj_cut, count(i))
                    sp.wait_ge(mn_made, count(i))
                    sp.dma_start(ADJ[:, :, :], adj_v[pair_index(prev(i, -1))]).then_inc(adj_in, 16)
                if Bs:
                    maximum_rows(0, b, 1 - par)
                if Cs:
                    for h in range(2):
                        sp.wait_ge(fin, count(c, h + 1, 2))
                        sp.dma_start(out_v[pair_index(c)][:, 2 * h:2 * h + 2, :],
                                     OUT[:, 2 * h:2 * h + 2, :]).then_inc(out_done, 16)
                if A and more:
                    sp.wait_ge(hp_x, count(i, 2, 2))
                    sp.dma_start(X[:, :, :], x_v[pair_index(prev(i, -1))]).then_inc(x_in, 16)
                if Bs:
                    maximum_rows(1, b, 1 - par)
                if A:
                    stack(0, i, par)
                    stack(1, i, par)

            pipeline(sp, body)
            sp.wait_ge(out_done, 2 * 16 * PAIRS)

        @block.gpsimd
        def _(pool):
            pool.memset(ident[:, :], 0.0).then_inc(c_made, 1)
            pool.memset(identb[:, :], 0.0).then_inc(c_made, 1)
            pool.memset(ones[:, :], 1.0).then_inc(c_made, 1)
            pool.memset(eps[:, :], EPS).then_inc(c_made, 1)
            pool.wait_ge(c_made, 4)
            for m in (ident, identb):
                pool.affine_select(out=m[:, :], in_=m[:, :], compare_op=ALU.not_equal, fill=1.0, base=0,
                                   pattern=[[-1, P]], channel_multiplier=1).then_inc(c_made, 1)
            pool.wait_ge(w_tr, 5)

            def over(column, n):
                return column.broadcast_to([P, T, n])

            def normalise(pair):
                pool.wait_ge(ln_rstd[0], count(pair))
                pool.wait_ge(h_t[3], count(prev(pair)))
                pool.tensor_tensor(XN[:, :, :], X[:, :, :], over(mv[:, :, 0:1], F), ALU.subtract).then_inc(xn_sub, 1)
                pool.wait_ge(xn_sub, count(pair))
                pool.tensor_tensor(XN[:, :, :], XN[:, :, :], over(rstd[:, :].rearrange("p (t u) -> p t u", u=1), F),
                                   ALU.mult).then_inc(ln_xn[0], 1)

            def split_c(a, pair, par):
                s = slice(a * N, (a + 1) * N)
                pool.wait_ge(c_hi, count(pair, a + 1, 2))
                pool.tensor_tensor(Cl[:, :, s], C[:, :, s], Ch[:, :, s].bitcast(f32), ALU.subtract).then_inc(c_lo, 1)
                if a == 0:
                    pool.wait_ge(r_t, count(prev(pair), 2, 2))
                pool.tensor_tensor(D[:, :, s], H2h[par][:, :, s].bitcast(f32), C[:, :, s], ALU.subtract).then_inc(d_sub, 1)
                pool.wait_ge(d_sub, count(pair, a + 1, 2))
                pool.tensor_tensor(D[:, :, s], D[:, :, s], H2l[par][:, :, s].bitcast(f32), ALU.add).then_inc(d_made, 1)

            def body(i, par, A, Bs, Cs, more):
                b, c = prev(i), prev(i, 2)
                if A:
                    normalise(i)
                if Cs:
                    split_c(1, c, par)
                if A:
                    pool.wait_ge(e0_max, count(i))
                    pool.tensor_tensor(E0[:, :, :], E0[:, :, :], over(WH[:, :, F + 1:F + 2], N), ALU.add).then_inc(e0_add, 1)
                    pool.wait_ge(e0_rinv, count(i))
                    pool.tensor_tensor(WH[:, :, 0:F], WH[:, :, 0:F], over(ri0[:, :].rearrange("p (t u) -> p t u", u=1), F),
                                       ALU.mult).then_inc(wh_norm, 1)
                    pool.wait_ge(x_in, count(i, 16, 16))
                    for h in range(2):
                        pool.wait_ge(hp_relu, count(i, h + 1, 2))
                        s = XN[:, 2 * h:2 * h + 2, :]
                        pool.tensor_tensor(s, s, X[:, 2 * h:2 * h + 2, :], ALU.add).then_inc(hp_x, 1)
                if Bs:
                    split_c(0, b, 1 - par)

            pipeline(pool, body)

        @block.scalar
        def _(act):
            act.preload_act_table_set("natural_log_exp_and_others")
            act.wait_ge(c_made, 6)
            srcs = [(S0, wqh), (S1, wkh), (T0, wvh)]
            for n, (ps, dst) in enumerate(srcs):
                act.wait_ge(w_tr, n + 1)
                act.activation(dst[:, :, :].rearrange("p f o -> p (f o)"), ps[:, :], ACT.Copy).then_inc(w_hi, 1)
            for n, ps in enumerate((BC, BR)):
                act.wait_ge(w_tr, 4 + n)
                act.activation(wgh[:, 2 * n:2 * n + 2, :].rearrange("p f o -> p (f o)"), ps[:, :], ACT.Copy).then_inc(w_hi, 1)
            act.wait_ge(wa_made, 4)
            act.activation(w0h[:, :, :], WH[:, 0:2, :], ACT.Copy).then_inc(w_hi, 1)
            act.wait_ge(bg_neg, 1)

            def inv_std(k, pair):
                act.wait_ge(ln_mv[k], count(pair))
                act.activation(rstd[:, :], mv[:, :, 1], ACT.Ln, bias=eps[:, 0:1]).then_inc(ln_log[k], 1)
                act.wait_ge(ln_log[k], count(pair))
                act.activation(rstd[:, :], rstd[:, :], ACT.Exp, scale=-0.5).then_inc(ln_rstd[k], 1)

            def relu_hi(layer, pair, dst, banks):
                for f in range(FT):
                    act.wait_ge(h_t[2 * layer + f], count(pair))
                    act.activation(dst[:, f, :], banks[f][:, :], ACT.Relu).then_inc(h_hi[2 * layer + f], 1)

            def exps(u, pair):
                act.wait_ge(st_mm[u % 4], of_unit(pair, u))
                if u >= PTS:
                    act.wait_ge(pv_mm, count(pair, (u - PTS) // 4 + 1, 4))
                else:
                    act.wait_ge(pv_mm, count(prev(pair), (max(w for w in range(UN) if w % PTS == u)) // 4 + 1, 4))
                act.activation(PT[u % PTS][:, :], TB[u % 2][:, :], ACT.Exp, scale=SCALE).then_inc(p_exp[u % 4], 1)

            def inv_sum(a, pair):
                act.wait_ge(pv_mm, count(pair, 2 * a + 2, 4))
                act.wait_ge(c_out, count(pair if a else prev(pair), 1 if a else 2, 2))
                act.activation(RI[:, :, :].rearrange("p f n -> p (f n)"), BR[:, :], ACT.Ln).then_inc(r_log, 1)
                act.wait_ge(r_log, count(pair, a + 1, 2))
                act.activation(RI[:, :, :], RI[:, :, :], ACT.Exp, scale=-1.0).then_inc(r_inv, 1)

            def c_high(a, pair):
                act.wait_ge(c_out, count(pair, a + 1, 2))
                act.activation(Ch[:, :, a * N:(a + 1) * N], C[:, :, a * N:(a + 1) * N], ACT.Copy).then_inc(c_hi, 1)

            def gate_exp(o, pair):
                act.wait_ge(z_mm, count(pair, o + 1, 2))
                act.activation(G[:, o, :], (BC, BR)[o][:, :], ACT.Exp, bias=nbg[:, o:o + 1], scale=-1.0).then_inc(z_exp, 1)

            def gate_log(o, pair):
                act.wait_ge(g_cut, count(pair, o + 1, 2))
                act.activation(G[:, o, :], G[:, o, :], ACT.Ln).then_inc(g_log, 1)

            def gate_inv(o, pair):
                act.wait_ge(g_log, count(pair, o + 1, 2))
                act.activation(G[:, o, :], G[:, o, :], ACT.Exp, scale=-1.0).then_inc(g_made, 1)

            def column_exps(pair):
                act.wait_ge(e0_leaky, count(pair))
                for t in range(T):
                    last = act.activation(E0[:, t, :], E0[:, t, :], ACT.Exp, bias=ngm[:, t:t + 1], accum_out=rs0[:, t:t + 1])
                last.then_inc(e0_exp, 1)

            def product_out(t, pair):
                act.wait_ge(wh_mm, count(pair, t + 1, 4))
                if t == 0:
                    act.wait_ge(stacked[0], count(prev(pair), 192, 192))
                act.activation(WH[:, t, :], (G1, G0)[t % 2][:, 0:F + 2], ACT.Copy).then_inc(wh_out, 1)

            def body(i, par, A, Bs, Cs, more):
                b, c = prev(i), prev(i, 2)
                if Cs:
                    for u in range(NH, NH + 3):
                        exps(u, c)
                if A:
                    inv_std(0, i)
                if Cs:
                    for u in range(NH + 3, UN):
                        exps(u, c)
                if A:
                    relu_hi(0, i, HTh, (G0, G1))
                if Cs:
                    inv_sum(1, c)
                if A:
                    act.wait_ge(adj_t, count(i))
                    act.activation(M1[par][:, :, :].rearrange("p t n -> p (t n)"), G0[:, :].bitcast(bf16), ACT.Copy).then_inc(clt_made, 1)
                if Cs:
                    c_high(1, c)
                if A:
                    for t in range(T):
                        product_out(t, i)
                if Cs:
                    gate_exp(0, c)
                    gate_log(0, c)
                    gate_inv(0, c)
                if A:
                    column_exps(i)
                if Cs:
                    gate_exp(1, c)
                if Bs:
                    exps(0, b)
                if Cs:
                    gate_log(1, c)
                if Bs:
                    exps(1, b)
                if Cs:
                    gate_inv(1, c)
                if Bs:
                    exps(2, b)
                    exps(3, b)
                if A:
                    for h in range(2):
                        act.wait_ge(hp_mm, count(i, h + 1, 2))
                        act.activation(XN[:, 2 * h:2 * h + 2, :].rearrange("p t f -> p (t f)"), (G0, G1)[h][:, :], ACT.Relu,
                                       scale=1.0 - SLOPE).then_inc(hp_relu, 1)
                if Bs:
                    for u in range(4, NH):
                        exps(u, b)
                if A:
                    inv_std(1, i)
                    relu_hi(1, i, H2h[par], (G0, G1))
                if Bs:
                    inv_sum(0, b)
                for n in range(4):
                    if A:
                        act.wait_ge(qk_mm, count(i, n + 1, 4))
                        act.activation(PR[n // 2][0][:, n % 2, :].bitcast(f32r), (G0, G1)[n % 2][:, :], ACT.Copy).then_inc(qk_hi, 1)
                    if n == 0 and Bs:
                        c_high(0, b)
                if A:
                    for n in range(2):
                        act.wait_ge(v_mm, count(i, n + 1, 2))
                        act.activation(V[par][:, 2 * n:2 * n + 2, :].rearrange("p t f -> p (t f)"), (G0, G1)[n][:, :], ACT.Copy).then_inc(v_out, 1)

            pipeline(act, body)

        @block.vector
        def _(dve):
            for k in range(2):
                last = dve.memset(KS[k][KR:KM, :, :].bitcast(f32), 1.0)
            last.then_inc(ks_ones, 1)
            dve.wait_ge(a_in, 48)
            for j in range(2):
                for f in range(FT):
                    dve.tensor_tensor_reduce(out=C[:, j, f * F:(f + 1) * F], in0=WH[:, f, 0:F], in1=E0[:, 2 + j, :], scale=1.0, scalar=0.0,
                                             op0=ALU.mult, op1=ALU.add, accum_out=WH[:, f, F + j:F + j + 1]).then_inc(wa_made, 1)
            dve.tensor_scalar(nbg[:, :], rstd[:, 0:2], -1.0, None, ALU.mult).then_inc(bg_neg, 1)
            for n, (ps, hi, lo) in enumerate(((S0, wqh, wql), (S1, wkh, wkl), (T0, wvh, wvl))):
                dve.wait_ge(w_hi, n + 1)
                dve.tensor_tensor(lo[:, :, :].rearrange("p f o -> p (f o)"), ps[:, :],
                                  hi[:, :, :].rearrange("p f o -> p (f o)").bitcast(f32), ALU.subtract).then_inc(w_lo, 1)
            for n, ps in enumerate((BC, BR)):
                dve.wait_ge(w_hi, 4 + n)
                dve.tensor_tensor(wgl[:, 2 * n:2 * n + 2, :].rearrange("p f o -> p (f o)"), ps[:, :],
                                  wgh[:, 2 * n:2 * n + 2, :].rearrange("p f o -> p (f o)").bitcast(f32), ALU.subtract).then_inc(w_lo, 1)
            dve.wait_ge(w_hi, 6)
            dve.wait_ge(wa_made, 4)
            dve.tensor_tensor(w0l[:, :, :], WH[:, 0:2, :], w0h[:, :, :].bitcast(f32), ALU.subtract).then_inc(w_lo, 1)
            dve.wait_ge(bg_neg, 1)

            def stats(k, src, pair, tiles):
                for t in tiles:
                    last = dve.bn_stats(bst[:, t, :], src[:, t, :])
                if t < T - 1:
                    return
                last.then_inc(ln_bst[k], 1)
                dve.wait_ge(ln_bst[k], count(pair))
                dve.wait_ge(ln_xn[1 - k], count(pair if k else prev(pair)))
                hold(dve, pair)
                for t in range(T):
                    last = dve.bn_aggr(mv[:, t, :], bst[:, t, :])
                last.then_inc(ln_mv[k], 1)

            def relu_lo(layer, pair, dst, hi, banks):
                for f in range(FT):
                    dve.wait_ge(h_hi[2 * layer + f], count(pair))
                    dve.scalar_tensor_tensor(out=dst[:, f, :], in0=banks[f][:, :], scalar=0.0, in1=hi[:, f, :].bitcast(f32),
                                             op0=ALU.max, op1=ALU.subtract).then_inc(h_lo[2 * layer + f], 1)

            def score_max(u, pair, par):
                a, h = u // NH, u % NH
                if u == 0:
                    dve.wait_ge(s_mm[u % 4], of_unit(pair, u))
                    dve.wait_ge(m_t, count(prev(pair), 2, 2))
                    hold(dve, pair)
                else:
                    dve.wait_ge(s_mm[u % 4], of_unit(pair, u))
                    hold(dve, pair)
                for t in range(2):
                    ps = SB[u % 2][:, t * N:(t + 1) * N]
                    last = dve.tensor_tensor_reduce(out=ps, in0=ps, in1=MN[par][:, 2 * a + t, :],
                                                    scale=-1.0, scalar=BIG, op0=ALU.add, op1=ALU.min,
                                                    accum_out=NM[:, 2 * a + t, h:h + 1])
                last.then_inc(s_max[u % 4], 1)

            def max_parts(a, pair, ps):
                dve.wait_ge(m_t, count(pair, a + 1, 2))
                dve.wait_ge(max_in[1 - a], count(pair if a else prev(pair), 32, 32))
                dve.tensor_copy(MH[:, :], ps[0:NH, 0:N]).then_inc(m_hi, 1)
                dve.wait_ge(m_hi, count(pair, a + 1, 2))
                dve.tensor_tensor(ML[:, :], ps[0:NH, 0:N], MH[:, :].bitcast(f32), ALU.subtract).then_inc(m_lo, 1)

            def attention_out(a, pair):
                dve.wait_ge(r_inv, count(pair, a + 1, 2))
                if a == 0:
                    dve.wait_ge(z_mm, count(prev(pair), 2, 2))
                    dve.wait_ge(r_made, count(prev(pair), 2, 2))
                    dve.wait_ge(c_lo, count(prev(pair), 2, 2))
                dve.tensor_tensor(C[:, :, a * N:(a + 1) * N], BC[:, :].rearrange("p (f n) -> p f n", f=FT), RI[:, :, :],
                                  ALU.mult).then_inc(c_out, 1)

            def gate_cut(o, pair):
                dve.wait_ge(z_exp, count(pair, o + 1, 2))
                dve.tensor_scalar(G[:, o, :], G[:, o, :], EMAX, 1.0, ALU.min, ALU.add).then_inc(g_cut, 1)

            def mix(o, pair):
                dve.wait_ge(d_made, count(pair, 2, 2))
                dve.wait_ge(g_made, count(pair, o + 1, 2))
                dve.tensor_tensor(D[:, o, :], D[:, o, :], G[:, o, :], ALU.mult).then_inc(gd_made, 1)
                dve.wait_ge(gd_made, count(pair, o + 1, 2))
                dve.tensor_tensor(D[:, o, :], D[:, o, :], C[:, o, :], ALU.add).then_inc(r_made, 1)

            def output(h, pair, par):
                dve.wait_ge(r_t, count(pair, h + 1, 2))
                if h == 0:
                    dve.wait_ge(out_done, count(prev(pair), 32, 32))
                dve.tensor_tensor(OUT[:, 2 * h:2 * h + 2, :].rearrange("p t f -> p (t f)"), (G0, G1)[h][:, :],
                                  X1[par][:, 2 * h:2 * h + 2, :].rearrange("p t f -> p (t f)"), ALU.add).then_inc(fin, 1)

            def residual(h, pair, par):
                dve.wait_ge(hp_x, count(pair, h + 1, 2))
                dve.scalar_tensor_tensor(out=X1[par][:, 2 * h:2 * h + 2, :].rearrange("p t f -> p (t f)"), in0=(G0, G1)[h][:, :],
                                         scalar=SLOPE, in1=XN[:, 2 * h:2 * h + 2, :].rearrange("p t f -> p (t f)"),
                                         op0=ALU.mult, op1=ALU.add).then_inc(x1_made, 1)

            def body(i, par, A, Bs, Cs, more):
                b, c = prev(i), prev(i, 2)
                bp = 1 - par
                if A:
                    dve.wait_ge(x_in, count(i, 16, 16))
                    stats(0, X, i, range(T))
                    dve.wait_ge(adj_in, count(i, 16, 16))
                    dve.wait_ge(adj_t, count(b))
                    dve.tensor_scalar(CL[:, :, :], ADJ[:, :, :], 1.0, -1.0, ALU.min, ALU.max).then_inc(adj_cut, 1)
                    for u in range(UN - 4, UN):
                        dve.wait_ge(s_max[u % 4], of_unit(c, u))
                    dve.tensor_scalar(MN[par][:, :, :], ADJ[:, :, :], 0.0, NEG, ALU.is_equal, ALU.mult).then_inc(mn_made, 1)
                    relu_lo(0, i, HTl, HTh, (G0, G1))
                if Cs:
                    attention_out(1, c)
                if A:
                    dve.wait_ge(clt_made, count(i))
                    dve.tensor_scalar(M0[:, :, :], M1[par][:, :, :], 0.0, NEG, ALU.is_le, ALU.mult).then_inc(m0_made, 1)
                if Bs:
                    dve.wait_ge(mn_made, count(b))
                    for u in range(0, 4):
                        score_max(u, b, bp)
                if A:
                    dve.wait_ge(m0_made, count(i))
                    dve.tensor_scalar(M1[par][:, :, :], M1[par][:, :, :], 0.0, NEG, ALU.is_equal, ALU.mult).then_inc(m1_made, 1)
                    dve.wait_ge(sib_t, count(i))
                    hold(dve, i)
                    for t in range(T):
                        a = t // 2
                        last = dve.tensor_tensor_reduce(out=E0[:, t, :], in0=G1[:, a * N:(a + 1) * N], in1=M0[:, t, :], scale=1.0,
                                                        scalar=-BIG, op0=ALU.add, op1=ALU.max, accum_out=mx0[:, t:t + 1])
                    last.then_inc(e0_max, 1)
                    dve.wait_ge(e0_max, count(i))
                    dve.scalar_tensor_tensor(out=nm0[:, :], in0=mx0[:, :], scalar=-1.0, in1=WH[:, :, F + 1], op0=ALU.mult,
                                             op1=ALU.subtract).then_inc(e0_nm, 1)
                    dve.wait_ge(e0_nm, count(i))
                    dve.scalar_tensor_tensor(out=ngm[:, :], in0=nm0[:, :], scalar=SLOPE, in1=nm0[:, :], op0=ALU.mult,
                                             op1=ALU.min).then_inc(e0_ngm, 1)
                if Bs:
                    for u in range(4, NH):
                        score_max(u, b, bp)
                if A:
                    dve.wait_ge(e0_ngm, count(i))
                    dve.wait_ge(e0_add, count(i))
                    e0 = E0[:, :, :].rearrange("p t n -> p (t n)")
                    dve.scalar_tensor_tensor(out=e0, in0=e0, scalar=SLOPE, in1=e0, op0=ALU.mult, op1=ALU.max).then_inc(e0_leaky, 1)
                if Bs:
                    max_parts(0, b, S0)
                if Cs:
                    gate_cut(0, c)
                    mix(0, c)
                if A:
                    dve.wait_ge(e0_exp, count(i))
                    dve.reciprocal(ri0[:, :], rs0[:, :]).then_inc(e0_rinv, 1)
                if Cs:
                    gate_cut(1, c)
                if Bs:
                    for u in range(NH, NH + 4):
                        score_max(u, b, bp)
                if Cs:
                    mix(1, c)
                    output(0, c, par)
                    output(1, c, par)
                if Bs:
                    score_max(NH + 4, b, bp)
                    score_max(NH + 5, b, bp)
                if A:
                    residual(0, i, par)
                    dve.wait_ge(x1_made, count(i, 1, 2))
                    stats(1, X1[par], i, (0, 1))
                    residual(1, i, par)
                    dve.wait_ge(x1_made, count(i, 2, 2))
                    stats(1, X1[par], i, (2, 3))
                if Bs:
                    score_max(NH + 6, b, bp)
                if A:
                    dve.wait_ge(ln_rstd[1], count(i))
                    for t in range(T):
                        last = dve.tensor_scalar(XN[:, t, :], X1[par][:, t, :], mv[:, t, 0:1], rstd[:, t:t + 1], ALU.subtract, ALU.mult)
                    last.then_inc(ln_xn[1], 1)
                if Bs:
                    score_max(NH + 7, b, bp)
                if A:
                    relu_lo(1, i, H2l[par], H2h[par], (G0, G1))
                if Bs:
                    max_parts(1, b, S0)
                for u in range(4):
                    if A:
                        dve.wait_ge(qk_hi, count(i, u + 1, 4))
                        dve.tensor_tensor(PR[u // 2][1][:, u % 2, :].bitcast(f32r), (G0, G1)[u % 2][:, :],
                                          PR[u // 2][0][:, u % 2, :], ALU.subtract).then_inc(qk_lo, 1)
                    if u == 0 and Bs:
                        attention_out(0, b)

            pipeline(dve, body)

        @block.tensor
        def _(pe):
            pe.wait_ge(c_made, 6)
            srcs = ((16, S0, XN[:, 0:2, :]), (32, S1, XN[:, 2:4, :]), (48, T0, E0[:, 0:2, :]),
                    (64, BC, G[:, :, 0:F]), (64, BR, G[:, :, F:2 * F]))
            pe.wait_ge(w_in, 64)
            for _, ps, src in srcs:
                for f in range(FT):
                    for o in range(FT):
                        last = pe.transpose(ps[:, f * F + o * P:f * F + (o + 1) * P], src[:, o, f * P:(f + 1) * P], ident[:, :])
                last.then_inc(w_tr, 1)
            pe.wait_ge(w_lo, 6)
            pe.wait_ge(ks_ones, 1)

            def split(ps, tiles, first, end, late=3, only=None):
                orders = (((0, 2), (1, 2)), ((0, 3),)) if late == 3 else (((0, 2), (0, 3)), ((1, 2),))
                for n, products_ in enumerate(orders):
                    if only is None or only == n:
                        for k, tile in enumerate(tiles):
                            for m, (l, r) in enumerate(products_):
                                last = pe.matmul(ps, tile[l], tile[r], start=first and n + k + m == 0,
                                                 stop=end and n == 1 and k == len(tiles) - 1)
                return last

            def feature_transposes(layer, f, ps):
                for t in range(T):
                    last = pe.transpose(ps[:, t * P:(t + 1) * P], XN[:, t, f * P:(f + 1) * P], ident[:, :])
                last.then_inc(h_t[2 * layer + f], 1)

            def scores(u, pair, par):
                a, h = u // NH, u % NH
                if u == 0:
                    for s in stacked:
                        pe.wait_ge(s, count(pair, 192, 192))
                if u % NH == 0:
                    pe.wait_ge(m_lo, count(pair if u else prev(pair), 1 if u else 2, 2))
                if u >= 2:
                    pe.wait_ge(s_max[(u - 2) % 4], of_unit(pair, u - 2))
                else:
                    pe.wait_ge(s_max[(UN + u - 2) % 4], of_unit(prev(pair), UN + u - 2))
                for t in range(2):
                    last = pe.matmul(SB[u % 2][:, t * N:(t + 1) * N], QS[par][0:KR, h, a * N + t * P:a * N + (t + 1) * P],
                                     KS[par][0:KR, h, a * N:(a + 1) * N], start=True, stop=True)
                last.then_inc(s_mm[u % 4], 1)

            def scores_t(u, pair, par):
                a, h = u // NH, u % NH
                if h == 0:
                    pe.wait_ge(max_in[a], count(pair, 32, 32))
                    pe.wait_ge(m1_made, count(pair))
                if u >= 2:
                    pe.wait_ge(p_exp[(u - 2) % 4], of_unit(pair, u - 2))
                else:
                    pe.wait_ge(p_exp[(UN + u - 2) % 4], of_unit(prev(pair), UN + u - 2))
                ps = TB[u % 2]
                pe.matmul(ps[:, :], identb[:, :], M1[par][:, 2 * a:2 * a + 2, :].rearrange("p t n -> p (t n)"),
                          start=True, stop=False)
                for t in range(2):
                    last = pe.matmul(ps[:, t * N:(t + 1) * N], KS[par][0:KM, h, a * N + t * P:a * N + (t + 1) * P],
                                     QS[par][0:KM, h, a * N:(a + 1) * N], start=False, stop=(t == 1))
                last.then_inc(st_mm[u % 4], 1)

            def weighted(g, pair, par):
                a, o = g // 2, g % 2
                if o == 0:
                    if a == 0:
                        pe.wait_ge(z_exp, count(prev(pair), 2, 2))
                    else:
                        pe.wait_ge(c_out, count(pair, 1, 2))
                for rhs_ones in (False, True):
                    ps = BR if rhs_ones else BC
                    for t in range(2):
                        for k in range(HG):
                            u = 4 * g + k
                            if t == 0 and not rhs_ones:
                                pe.wait_ge(p_exp[u % 4], of_unit(pair, u))
                            lhs = ones[:, :] if rhs_ones else V[par][:, 2 * a + t, o * P + k * DK:o * P + (k + 1) * DK]
                            last = pe.matmul(ps[k * DK:(k + 1) * DK, o * N:(o + 1) * N], lhs, PT[u % PTS][:, t * N:(t + 1) * N],
                                             start=(t == 0), stop=(t == 1))
                last.then_inc(pv_mm, 1)

            def max_transposes(a, pair):
                for u in range(NH * a + 4, NH * a + NH):
                    pe.wait_ge(s_max[u % 4], of_unit(pair, u))
                for t in range(2):
                    last = pe.transpose(S0[0:NH, t * P:(t + 1) * P], NM[:, 2 * a + t, :], ident[:, :])
                last.then_inc(m_t, 1)

            def gate(o, half, par, only=None):
                hi, lo = (H2h[par], H2l[par]) if half == "x" else (Ch, Cl)
                k = FT if half == "x" else 0
                return split((BC, BR)[o][:, :], [(wgh[:, f + k, o * P:(o + 1) * P], wgl[:, f + k, o * P:(o + 1) * P],
                                                  hi[:, f, :], lo[:, f, :]) for f in range(FT)],
                             half == "x", half == "c", only=only)

            def products(t, pair):
                s = slice(t * P, (t + 1) * P)
                split((G1, G0)[t % 2][:, 0:F + 2], [(HTh[:, f, s], HTl[:, f, s], w0h[:, f, :], w0l[:, f, :]) for f in range(FT)],
                      True, True).then_inc(wh_mm, 1)

            def body(i, par, A, Bs, Cs, more):
                b, c = prev(i), prev(i, 2)
                bp = 1 - par
                if Cs:
                    for u in range(NH, UN):
                        scores_t(u, c, par)
                        if u == NH + 5:
                            pe.wait_ge(v_out, count(c, 2, 2))
                            weighted(2, c, par)
                if A:
                    pe.wait_ge(ln_xn[0], count(i))
                    for f in range(FT):
                        pe.wait_ge(v_out, count(b, f + 1, 2))
                        feature_transposes(0, f, (G0, G1)[f])
                if Cs:
                    weighted(3, c, par)
                if A:
                    pe.wait_ge(adj_cut, count(i))
                    pe.wait_ge(h_lo[0], count(i))
                    for t in range(T):
                        for j in range(2):
                            at = ((t // 2) * 2 + j) * N + (t % 2) * P
                            last = pe.transpose(G0[:, :].bitcast(bf16)[:, at:at + P], CL[:, t, j * P:(j + 1) * P], identb[:, :])
                    last.then_inc(adj_t, 1)
                for t in range(T):
                    if A:
                        if t == 0:
                            pe.wait_ge(h_lo[1], count(i))
                        elif t == 1:
                            pe.wait_ge(clt_made, count(i))
                        else:
                            pe.wait_ge(wh_out, count(i, t - 1, 4))
                        products(t, i)
                    if Bs:
                        scores(t, b, bp)
                if A:
                    for t in range(T):
                        pe.wait_ge(wh_out, count(i, max(t + 1, 3), 4))
                        last = pe.transpose(G1[:, t * P:(t + 1) * P], WH[:, t, F:F + 1].broadcast_to([P, P]), ident[:, :])
                    last.then_inc(sib_t, 1)
                if Bs:
                    scores(4, b, bp)
                    scores(5, b, bp)
                if Cs:
                    pe.wait_ge(c_out, count(c, 2, 2))
                    gate(0, "x", par)
                if Bs:
                    scores(6, b, bp)
                    scores(7, b, bp)
                if Cs:
                    pe.wait_ge(c_hi, count(c, 2, 2))
                    gate(0, "c", par, only=0)
                    pe.wait_ge(c_lo, count(c, 2, 2))
                    gate(0, "c", par, only=1).then_inc(z_mm, 1)
                if Bs:
                    max_transposes(0, b)
                if Cs:
                    gate(1, "x", par)
                    gate(1, "c", par).then_inc(z_mm, 1)
                if Bs:
                    for n in range(4):
                        scores_t(n, b, bp)
                        scores(NH + n, b, bp)
                    pe.wait_ge(v_out, count(b, 2, 2))
                    weighted(0, b, bp)
                if Cs:
                    for h in range(2):
                        if h == 0:
                            pe.wait_ge(r_made, count(c, 2, 2))
                            if A:
                                pe.wait_ge(wh_out, count(i, 4, 4))
                        elif A:
                            pe.wait_ge(e0_max, count(i))
                        for t in (2 * h, 2 * h + 1):
                            for f in range(FT):
                                last = pe.transpose((G0, G1)[h][:, (t % 2) * F + f * P:(t % 2) * F + (f + 1) * P],
                                                    D[:, f, t * P:(t + 1) * P], ident[:, :])
                        last.then_inc(r_t, 1)
                if A:
                    pe.wait_ge(wh_norm, count(i))
                    for a in range(2):
                        pe.wait_ge(fin, count(c, a + 1, 2))
                        for t in range(2):
                            for j in range(2):
                                last = pe.matmul((G0, G1)[a][:, t * F:(t + 1) * F], E0[:, 2 * a + j, t * P:(t + 1) * P],
                                                 WH[:, 2 * a + j, 0:F], start=(j == 0), stop=(j == 1))
                        last.then_inc(hp_mm, 1)
                if Bs:
                    for n in range(4, NH):
                        scores_t(n, b, bp)
                        scores(NH + n, b, bp)
                    weighted(1, b, bp)
                if A:
                    pe.wait_ge(ln_xn[1], count(i))
                    for f in range(FT):
                        pe.wait_ge(x1_made, count(i, f + 1, 2))
                        feature_transposes(1, f, (G0, G1)[f])
                if Bs:
                    max_transposes(1, b)
                if A:
                    pe.wait_ge(h_hi[2], count(i))
                    pe.wait_ge(h_hi[3], count(i))
                    for n in range(4):
                        ps, o = (G0, G1)[n % 2], n % 2
                        if n < 2:
                            pe.wait_ge(h_lo[2 + n], count(i))
                        else:
                            pe.wait_ge(qk_lo, count(i, n - 1, 4))
                        wh_, wl_ = ((wqh, wql), (wkh, wkl))[n // 2]
                        tiles = [(wh_[:, f, o * P:(o + 1) * P], wl_[:, f, o * P:(o + 1) * P], H2h[par][:, f, :], H2l[par][:, f, :])
                                 for f in range(FT)]
                        split(ps[:, :], tiles, True, True, only=0)
                        if n == 0:
                            pe.wait_ge(h_lo[3], count(i))
                        split(ps[:, :], tiles, True, True, only=1).then_inc(qk_mm, 1)
                    for n in range(2):
                        pe.wait_ge(qk_lo, count(i, n + 3, 4))
                        for t in (2 * n, 2 * n + 1):
                            s = slice(t * P, (t + 1) * P)
                            last = split((G0, G1)[n][:, (t % 2) * F:(t % 2 + 1) * F],
                                         [(H2h[par][:, f, s], H2l[par][:, f, s], wvh[:, f, :], wvl[:, f, :]) for f in range(FT)], True, True)
                        last.then_inc(v_mm, 1)

            pipeline(pe, body)


_INS = ["x", "adj", "L0_gnn_W", "L0_gnn_a", "L1_gnn_Wq", "L1_gnn_Wk", "L1_gnn_Wv", "L1_gnn_Wg", "L1_gnn_bg"]


def kernel(**inputs):
    import numpy as _np
    import concourse.bacc as _bacc
    from concourse import mybir as _mybir
    from concourse.bass_utils import run_bass_kernel_spmd as _run

    nc = _bacc.Bacc("TRN2", target_bir_lowering=False, num_devices=1)
    arrays, args = {}, []
    for name in _INS:
        a = _np.ascontiguousarray(inputs[name])
        arrays[f"in_{name}"] = a
        args.append(nc.dram_tensor(f"in_{name}", a.shape, _mybir.dt.from_np(a.dtype), kind="ExternalInput").ap())
    shape = inputs["x"].shape
    args.append(nc.dram_tensor("out_dram", shape, _mybir.dt.from_np(_np.dtype("float32")), kind="ExternalOutput").ap())
    gnn_kernel(nc, *args)
    r = _run(nc, [arrays], core_ids=[0])
    return r.results[0]["out_dram"]
```

```python
import concourse.bass as bass
from concourse import mybir
from contextlib import ExitStack


def gnn_kernel(nc: bass.Bass, x, adj, w0, a0, wq, wk, wv, wg, bg, out):
    f32, f32r, bf16, i32 = mybir.dt.float32, mybir.dt.float32r, mybir.dt.bfloat16, mybir.dt.int32
    ALU = mybir.AluOpType
    ACT = mybir.ActivationFunctionType

    B, N, F = x.shape
    P = 128
    NH = 8
    DK = F // NH
    PAIRS = B // 2
    T = 2 * N // P
    NT = 2 * N
    FT = F // P
    HG = P // DK
    UN = 2 * NH
    NEG = -1e30
    BIG = 3e38
    SLOPE = 0.2
    EPS = 1e-5
    EMAX = 1e18
    SCALE = float(DK) ** -0.5
    KR = 3 * DK
    KM = KR + 2
    FIRST = 3
    HEADS = [g + HG * f for g in range(HG) for f in range(FT)]
    PTS = 6

    x_v = x.rearrange("(n a) (i p) c -> n p (a i) c", a=2, p=P)
    adj_v = adj.rearrange("(n a) (i p) c -> n p (a i) c", a=2, p=P)
    out_v = out.rearrange("(n a) (i p) c -> n p (a i) c", a=2, p=P)

    ctx = ExitStack()
    with ctx:
        def sb(name, shape, dt):
            return ctx.enter_context(nc.sbuf_tensor(name, shape, dt))

        def sem(name):
            return ctx.enter_context(nc.semaphore(name))

        def sems(name, n):
            return [sem(f"{name}{k}") for k in range(n)]

        ident = sb("ident", [P, P], f32)
        identb = sb("identb", [P, P], bf16)
        ones = sb("ones", [P, DK], f32)
        w0h, w0l = sb("w0h", [P, FT, F + 2], f32r), sb("w0l", [P, FT, F + 2], f32r)
        wqh, wql = sb("wqh", [P, FT, F], f32r), sb("wql", [P, FT, F], f32r)
        wkh, wkl = sb("wkh", [P, FT, F], f32r), sb("wkl", [P, FT, F], f32r)
        wvh, wvl = sb("wvh", [P, FT, F], f32r), sb("wvl", [P, FT, F], f32r)
        wgh, wgl = sb("wgh", [P, 2 * FT, F], f32r), sb("wgl", [P, 2 * FT, F], f32r)
        nbg = sb("nbg", [P, FT], f32)
        eps = sb("eps", [P, 1], f32)
        tiny = sb("tiny", [1, 64], f32)
        X = sb("X", [P, T, F], f32)
        ADJ = sb("ADJ", [P, T, N], i32)
        CL = sb("CL", [P, T, N], bf16)
        CLT = sb("CLT", [P, T, N], bf16)
        M1 = [sb(f"M1_{k}", [P, T, N], bf16) for k in range(2)]
        MN = [sb(f"MN_{k}", [P, T, N], bf16) for k in range(2)]
        XN = sb("XN", [P, T, F], f32)
        HTh, HTl = sb("HTh", [P, FT, NT], f32r), sb("HTl", [P, FT, NT], f32r)
        WH = sb("WH", [P, T, F + 2], f32)
        E0 = sb("E0", [P, T, N], f32)
        OUT = sb("OUT", [P, T, F], f32)
        X1 = [sb(f"X1_{k}", [P, T, F], f32) for k in range(2)]
        H2h = [sb(f"H2h_{k}", [P, FT, NT], f32r) for k in range(2)]
        H2l = [sb(f"H2l_{k}", [P, FT, NT], f32r) for k in range(2)]
        PRK = sb("PRK", [P, FT, NT], f32)
        QS = [sb(f"QS_{k}", [P, NH, NT], f32r) for k in range(2)]
        KS = [sb(f"KS_{k}", [P, NH, NT], f32r) for k in range(2)]
        V = [sb(f"V_{k}", [P, T, F], f32) for k in range(2)]
        bst = sb("bst", [P, T, 6], f32)
        mv = sb("mv", [P, T, 2], f32)
        rstd = sb("rstd", [P, T], f32)
        mx0 = sb("mx0", [P, T], f32)
        nm0 = sb("nm0", [P, T], f32)
        nmr = sb("nmr", [P, T], f32)
        ngm = sb("ngm", [P, T], f32)
        rs0 = sb("rs0", [P, T], f32)
        ri0 = sb("ri0", [P, T], f32)
        NM = sb("NM", [P, T, NH], f32)
        MH, ML = sb("MH", [NH, N], f32r), sb("ML", [NH, N], f32r)
        PT = [sb(f"PT{k}", [P, 2 * N], f32) for k in range(PTS)]
        RI = sb("RI", [P, FT, N], f32)
        C = sb("C", [P, FT, NT], f32)
        Ch, Cl = sb("Ch", [P, FT, NT], f32r), sb("Cl", [P, FT, NT], f32r)
        D = sb("D", [P, FT, NT], f32)
        G = sb("G", [P, FT, NT], f32)
        PR = [[WH[:, :, :].rearrange("p t f -> p (t f)")[:, 0:FT * NT].rearrange("p (f n) -> p f n", f=FT),
               E0[:, :, :].rearrange("p (f t) n -> p f (t n)", f=FT)],
              [PRK[:, :, :], G[:, :, :]]]

        def bank(name):
            return ctx.enter_context(nc.psum_tensor(name, [P, 512], f32))

        G0, G1, S0, S1, T0, T1, BC, BR = [bank(n) for n in ("G0", "G1", "S0", "S1", "T0", "T1", "BC", "BR")]
        SB, TB = [S0, S1], [T0, T1]

        c_made, a_in, wa_made, w_tr, w_hi, w_lo, ks_ones, bg_neg = [
            sem(n) for n in ("c_made", "a_in", "wa_made", "w_tr", "w_hi", "w_lo", "ks_ones", "bg_neg")]
        w_in = sems("w_in", 4)
        x_in, adj_in, out_done = sem("x_in"), sem("adj_in"), sem("out_done")
        stacked = [sems(n, HG) for n in ("q_stacked", "k_stacked")]
        max_in = sems("max_in", 2)
        ln_bst, ln_mv, ln_log, ln_rstd, ln_xn = [sems(n, 2) for n in ("ln_bst", "ln_mv", "ln_log", "ln_rstd", "ln_xn")]
        h_t, h_hi, h_lo = sems("h_t", 4), sems("h_hi", 4), sems("h_lo", 4)
        xn_sub, ln_nmr = sem("xn_sub"), sem("ln_nmr")
        adj_cut, mn_made, adj_t, clt_made, m0_made, m1_made = [
            sem(n) for n in ("adj_cut", "mn_made", "adj_t", "clt_made", "m0_made", "m1_made")]
        wh_mm, wh_out, sib_t, e0_max, e0_nm, e0_ngm, e0_add, e0_leaky, e0_exp, e0_rinv, wh_norm = [
            sem(n) for n in ("wh_mm", "wh_out", "sib_t", "e0_max", "e0_nm", "e0_ngm", "e0_add", "e0_leaky", "e0_exp", "e0_rinv", "wh_norm")]
        x1_kept = sem("x1_kept")
        hp_mm, hp_relu, hp_x, x1_made = [sem(n) for n in ("hp_mm", "hp_relu", "hp_x", "x1_made")]
        qk_mm, qk_hi, qk_lo = sem("qk_mm"), sem("qk_hi"), sem("qk_lo")
        v_mm, v_out = sem("v_mm"), sem("v_out")
        s_mm, s_max = sems("s_mm", 4), sems("s_max", 4)
        m_t, m_hi, m_lo = sem("m_t"), sem("m_hi"), sem("m_lo")
        st_mm, p_exp = sems("st_mm", 4), sems("p_exp", 4)
        pv_mm = sem("pv_mm")
        r_log, r_inv, c_out, c_hi, c_lo, d_sub, d_made = [
            sem(n) for n in ("r_log", "r_inv", "c_out", "c_hi", "c_lo", "d_sub", "d_made")]
        z_mm, z_exp = sem("z_mm"), sem("z_exp")
        g_cut, g_log, g_made, gd_made, r_made = [sem(n) for n in ("g_cut", "g_log", "g_made", "gd_made", "r_made")]
        r_t, fin = sem("r_t"), sem("fin")

        def count(pair, k=1, per=1):
            base, off = pair
            c = off * per + k
            if base is None:
                return c if off >= 0 else 0
            signals = base if per == 1 else base * per
            return signals + c if c else signals

        def of_unit(pair, u):
            return count(pair, u // 4 + 1, 4)

        held = [0]

        def hold(dve, pair):
            if pair[0] is not None:
                held[0] = (held[0] + 1) % 64
                dve.memset(tiny[:, held[0]:held[0] + 1], 0.0)

        def pipeline(eng, body):
            for n in range(FIRST):
                body((None, n), n % 2, n >= 0, n >= 1, n >= 2, True)
            with eng.Fori(FIRST, PAIRS - 2, 2) as i:
                for d in (0, 1):
                    body((i, d), (FIRST + d) % 2, True, True, True, True)
            for n in range(PAIRS - 1, PAIRS + 2):
                body((None, n), n % 2, n < PAIRS, n <= PAIRS, True, n + 1 < PAIRS)

        def following(pair):
            return pair[0], pair[1] + 1

        def prev(pair, n=1):
            return pair[0], pair[1] - n

        def pair_index(pair):
            base, off = pair
            return off if base is None else base + off if off else base

        block = ctx.enter_context(nc.Block())

        @block.sync
        def _(sp):
            stage = {"wq": D[:, 0, :], "wk": D[:, 1, :], "wv": E0[:, 0:2, :].rearrange("p f c -> p (f c)")}
            sp.dma_start(X[:, :, :], x_v[0]).then_inc(x_in, 16)
            sp.dma_start(ADJ[:, :, :], adj_v[0]).then_inc(adj_in, 16)
            sp.dma_start(WH[:, 0:2, 0:F], w0.rearrange("(f p) o -> p f o", p=P)).then_inc(a_in, 16)
            sp.dma_start(E0[:, 2:4, :], a0.rearrange("(j o) u -> u j o", j=2).broadcast_to([P, 2, F])).then_inc(a_in, 16)
            with nc.allow_non_contiguous_dma(reason="256 numbers, once"):
                sp.dma_start(nmr[:, 0:2], bg.rearrange("(f p) -> p f", p=P)).then_inc(a_in, 16)

            for n, (name, w) in enumerate((("wq", wq), ("wk", wk), ("wv", wv))):
                sp.dma_start(stage[name].rearrange("p (f c) -> p f c", f=FT), w.rearrange("(f p) c -> p f c", p=P)).then_inc(w_in[n], 16)
            sp.dma_start(G[:, :, :], wg.rearrange("(f p) c -> p f c", p=P)).then_inc(w_in[3], 16)

            def maximum_rows(a, pair, par):
                sp.wait_ge(m_hi, count(pair, a + 1, 2))
                sp.dma_start(QS[par][KR:KR + 1, :, a * N:(a + 1) * N].bitcast(f32), MH[:, :].bitcast(f32)).then_inc(max_in[a], 16)
                sp.wait_ge(m_lo, count(pair, a + 1, 2))
                sp.dma_start(QS[par][KR + 1:KR + 2, :, a * N:(a + 1) * N].bitcast(f32), ML[:, :].bitcast(f32)).then_inc(max_in[a], 16)

            def stack(n, pair, par, between=None):
                dst, parts = ((QS, (0, 0, 1)), (KS, (0, 1, 0)))[n]
                sp.wait_ge(qk_hi, count(pair, 2 * n + 2, 4))
                sp.wait_ge(qk_lo, count(pair, 2 * n + 2, 4))
                for g in range(HG):
                    for j in range(3):
                        sp.dma_start(dst[par][j * DK:(j + 1) * DK, g:NH:HG, :].bitcast(f32),
                                     PR[n][parts[j]][g * DK:(g + 1) * DK, :, :]).then_inc(stacked[n][g], 16)
                    if g == 1 and between is not None:
                        maximum_rows(1, between, 1 - par)

            def body(i, par, A, Bs, Cs, more):
                b, c = prev(i), prev(i, 2)
                if A and more:
                    sp.wait_ge(adj_cut, count(i))
                    sp.wait_ge(mn_made, count(i))
                    sp.dma_start(ADJ[:, :, :], adj_v[pair_index(following(i))]).then_inc(adj_in, 16)
                if Bs:
                    maximum_rows(0, b, 1 - par)
                if Cs:
                    for h in range(2):
                        sp.wait_ge(fin, count(c, h + 1, 2))
                        sp.dma_start(out_v[pair_index(c)][:, 2 * h:2 * h + 2, :],
                                     OUT[:, 2 * h:2 * h + 2, :]).then_inc(out_done, 16)
                if A and more:
                    sp.wait_ge(x1_kept, count(i))
                    sp.dma_start(X[:, :, :], x_v[pair_index(following(i))]).then_inc(x_in, 16)
                if A:
                    stack(0, i, par, b if Bs else None)
                    stack(1, i, par)
                elif Bs:
                    maximum_rows(1, b, 1 - par)

            pipeline(sp, body)
            sp.wait_ge(out_done, 2 * 16 * PAIRS)

        @block.gpsimd
        def _(pool):
            pool.memset(ident[:, :], 0.0).then_inc(c_made, 1)
            pool.memset(identb[:, :], 0.0).then_inc(c_made, 1)
            pool.memset(ones[:, :], 1.0).then_inc(c_made, 1)
            pool.memset(eps[:, :], EPS).then_inc(c_made, 1)
            pool.wait_ge(c_made, 4)
            for m in (ident, identb):
                pool.affine_select(out=m[:, :], in_=m[:, :], compare_op=ALU.not_equal, fill=1.0, base=0,
                                   pattern=[[-1, P]], channel_multiplier=1).then_inc(c_made, 1)
            pool.wait_ge(c_made, 6)
            for k in range(2):
                pool.memset(KS[k][KR:KM, :, :].bitcast(f32), 1.0).then_inc(ks_ones, 1)
            pool.wait_ge(ks_ones, 2)

            def over(column, n):
                return column.broadcast_to([P, T, n])

            def normalise(pair):
                pool.wait_ge(ln_rstd[0], count(pair))
                pool.wait_ge(h_t[3], count(prev(pair)))
                pool.tensor_tensor(XN[:, :, :], X[:, :, :], over(mv[:, :, 0:1], F), ALU.subtract).then_inc(xn_sub, 1)
                pool.wait_ge(xn_sub, count(pair))
                pool.tensor_tensor(XN[:, :, :], XN[:, :, :], over(rstd[:, :].rearrange("p (t u) -> p t u", u=1), F),
                                   ALU.mult).then_inc(ln_xn[0], 1)

            def c_low(a, pair):
                s = slice(a * N, (a + 1) * N)
                pool.wait_ge(c_hi, count(pair, a + 1, 2))
                pool.tensor_tensor(Cl[:, :, s], C[:, :, s], Ch[:, :, s].bitcast(f32), ALU.subtract).then_inc(c_lo, 1)

            def mix_product(o, pair):
                pool.wait_ge(d_made, count(pair, 2, 2))
                pool.wait_ge(g_made, count(pair, o + 1, 2))
                pool.tensor_tensor(D[:, o, :], D[:, o, :], G[:, o, :], ALU.mult).then_inc(gd_made, 1)

            def difference(a, pair, par):
                s = slice(a * N, (a + 1) * N)
                if a == 0:
                    pool.wait_ge(r_t, count(prev(pair), 2, 2))
                pool.tensor_tensor(D[:, :, s], H2h[par][:, :, s].bitcast(f32), C[:, :, s], ALU.subtract).then_inc(d_sub, 1)
                pool.wait_ge(d_sub, count(pair, a + 1, 2))
                pool.tensor_tensor(D[:, :, s], D[:, :, s], H2l[par][:, :, s].bitcast(f32), ALU.add).then_inc(d_made, 1)

            def body(i, par, A, Bs, Cs, more):
                b, c = prev(i), prev(i, 2)
                if Cs:
                    c_low(1, c)
                if A:
                    for a in range(2):
                        pool.wait_ge(e0_rinv, count(i, a + 1, 2))
                        pool.tensor_tensor(WH[:, 2 * a:2 * a + 2, 0:F], WH[:, 2 * a:2 * a + 2, 0:F],
                                           ri0[:, 2 * a:2 * a + 2].rearrange("p (t u) -> p t u", u=1).broadcast_to([P, 2, F]),
                                           ALU.mult).then_inc(wh_norm, 1)
                if Cs:
                    difference(1, c, par)
                if A:
                    for h in range(2):
                        pool.wait_ge(hp_x, count(i, h + 1, 2))
                        s = slice(2 * h, 2 * h + 2)
                        pool.tensor_tensor(X[:, s, :], X[:, s, :], XN[:, s, :], ALU.add).then_inc(x1_made, 1)
                if Cs:
                    mix_product(0, c)
                    mix_product(1, c)
                if more:
                    normalise(following(i))
                if Bs:
                    c_low(0, b)
                    difference(0, b, 1 - par)

            normalise((None, 0))
            pipeline(pool, body)

        @block.scalar
        def _(act):
            act.preload_act_table_set("natural_log_exp_and_others")
            act.wait_ge(c_made, 6)
            def inv_std(k, pair):
                act.wait_ge(ln_mv[k], count(pair))
                act.activation(rstd[:, :], mv[:, :, 1], ACT.Ln, bias=eps[:, 0:1]).then_inc(ln_log[k], 1)
                act.wait_ge(ln_log[k], count(pair))
                act.activation(rstd[:, :], rstd[:, :], ACT.Exp, scale=-0.5).then_inc(ln_rstd[k], 1)

            inv_std(0, (None, 0))
            srcs = [(S0, wqh), (S1, wkh), (T0, wvh)]
            for n, (ps, dst) in enumerate(srcs):
                act.wait_ge(w_tr, n + 1)
                act.activation(dst[:, :, :].rearrange("p f o -> p (f o)"), ps[:, :], ACT.Copy).then_inc(w_hi, 1)
            for n, ps in enumerate((BC, BR)):
                act.wait_ge(w_tr, 4 + n)
                act.activation(wgh[:, 2 * n:2 * n + 2, :].rearrange("p f o -> p (f o)"), ps[:, :], ACT.Copy).then_inc(w_hi, 1)
            act.wait_ge(wa_made, 4)
            act.activation(w0h[:, :, :], WH[:, 0:2, :], ACT.Copy).then_inc(w_hi, 1)
            act.wait_ge(bg_neg, 1)

            def relu_hi(layer, f, pair, dst):
                act.wait_ge(h_t[2 * layer + f], count(pair))
                act.activation(dst[:, f, :], (G0, G1)[f][:, :], ACT.Relu).then_inc(h_hi[2 * layer + f], 1)

            def exps(u, pair):
                act.wait_ge(st_mm[u % 4], of_unit(pair, u))
                if u >= PTS:
                    act.wait_ge(pv_mm, count(pair, (u - PTS) // 4 + 1, 4))
                else:
                    act.wait_ge(pv_mm, count(prev(pair), (max(w for w in range(UN) if w % PTS == u)) // 4 + 1, 4))
                act.activation(PT[u % PTS][:, :], TB[u % 2][:, :], ACT.Exp, scale=SCALE).then_inc(p_exp[u % 4], 1)

            def inv_sum(a, pair):
                act.wait_ge(pv_mm, count(pair, 2 * a + 2, 4))
                act.wait_ge(c_out, count(pair if a else prev(pair), 1 if a else 2, 2))
                act.activation(RI[:, :, :].rearrange("p f n -> p (f n)"), BR[:, :], ACT.Ln).then_inc(r_log, 1)
                act.wait_ge(r_log, count(pair, a + 1, 2))
                act.activation(RI[:, :, :], RI[:, :, :], ACT.Exp, scale=-1.0).then_inc(r_inv, 1)

            def c_high(a, pair):
                act.wait_ge(c_out, count(pair, a + 1, 2))
                act.activation(Ch[:, :, a * N:(a + 1) * N], C[:, :, a * N:(a + 1) * N], ACT.Copy).then_inc(c_hi, 1)

            def gate_exp(o, pair):
                act.wait_ge(z_mm, count(pair, o + 1, 2))
                act.activation(G[:, o, :], (BC, BR)[o][:, :], ACT.Exp, bias=nbg[:, o:o + 1], scale=-1.0).then_inc(z_exp, 1)

            def gate_log(o, pair):
                act.wait_ge(g_cut, count(pair, o + 1, 2))
                act.activation(G[:, o, :], G[:, o, :], ACT.Ln).then_inc(g_log, 1)

            def gate_inv(o, pair):
                act.wait_ge(g_log, count(pair, o + 1, 2))
                act.activation(G[:, o, :], G[:, o, :], ACT.Exp, scale=-1.0).then_inc(g_made, 1)

            def column_mask(t, pair):
                act.wait_ge(wh_out, count(pair, t + 1, 4))
                act.activation(E0[:, t, :], E0[:, t, :], ACT.Identity, bias=WH[:, t, F + 1:F + 2]).then_inc(e0_add, 1)

            def column_exps(a, pair):
                act.wait_ge(e0_leaky, count(pair, a + 1, 2))
                for t in (2 * a, 2 * a + 1):
                    last = act.activation(E0[:, t, :], E0[:, t, :], ACT.Exp, bias=ngm[:, t:t + 1], accum_out=rs0[:, t:t + 1])
                last.then_inc(e0_exp, 1)

            def value_out(n, pair, par):
                act.wait_ge(v_mm, count(pair, n + 1, 2))
                act.activation(V[par][:, 2 * n:2 * n + 2, :].rearrange("p t f -> p (t f)"), (G0, G1)[n][:, :], ACT.Copy).then_inc(v_out, 1)

            def qk_high(n, pair):
                act.wait_ge(qk_mm, count(pair, n + 1, 4))
                act.activation(PR[n // 2][0][:, n % 2, :].bitcast(f32r), (G0, G1)[n % 2][:, :], ACT.Copy).then_inc(qk_hi, 1)

            def product_out(t, pair):
                act.wait_ge(wh_mm, count(pair, t + 1, 4))
                if t == 0:
                    for g in range(HG):
                        act.wait_ge(stacked[0][g], count(prev(pair), 48, 48))
                act.activation(WH[:, t, :], (G1, G0)[t % 2][:, 0:F + 2], ACT.Copy).then_inc(wh_out, 1)

            def body(i, par, A, Bs, Cs, more):
                b, c = prev(i), prev(i, 2)
                if Bs:
                    value_out(0, b, 1 - par)
                    value_out(1, b, 1 - par)
                for n in range(8):
                    if Cs:
                        exps(NH + n, c)
                        if n == 4:
                            c_high(0, c)
                    if A and n in (1, 2):
                        relu_hi(0, n - 1, i, HTh)
                    if A and n == 4:
                        act.wait_ge(adj_t, count(i))
                        act.wait_ge(m1_made, count(b))
                        act.activation(CLT[:, :, :].rearrange("p t n -> p (t n)"), G0[:, :].bitcast(bf16), ACT.Copy).then_inc(clt_made, 1)
                    if A and n > 4:
                        product_out(n - 5, i)
                if A:
                    act.wait_ge(m0_made, count(i))
                    for t in range(T - 1):
                        column_mask(t, i)
                if Cs:
                    inv_sum(1, c)
                if A:
                    product_out(3, i)
                    column_mask(3, i)
                if Cs:
                    c_high(1, c)
                if A:
                    column_exps(0, i)
                    column_exps(1, i)
                if Bs:
                    for g in range(HG):
                        act.wait_ge(stacked[1][g], count(b, 48, 48))
                if Cs:
                    gate_exp(0, c)
                    gate_exp(1, c)
                    gate_log(0, c)
                    gate_inv(0, c)
                for h in range(2):
                    if h and Cs:
                        gate_log(1, c)
                        gate_inv(1, c)
                    if A:
                        act.wait_ge(hp_mm, count(i, h + 1, 2))
                        act.activation(XN[:, 2 * h:2 * h + 2, :].rearrange("p t f -> p (t f)"), (G0, G1)[h][:, :], ACT.Relu,
                                       scale=1.0 - SLOPE).then_inc(hp_relu, 1)
                if Bs:
                    exps(0, b)
                    exps(1, b)
                    exps(2, b)
                    exps(3, b)
                    exps(4, b)
                if A:
                    inv_std(1, i)
                    act.wait_ge(ln_nmr, count(i))
                    for t in range(T):
                        last = act.activation(XN[:, t, :], X[:, t, :], ACT.Identity, bias=nmr[:, t:t + 1], scale=rstd[:, t:t + 1])
                    last.then_inc(ln_xn[1], 1)
                    relu_hi(1, 0, i, H2h[par])
                    relu_hi(1, 1, i, H2h[par])
                if Bs:
                    exps(5, b)
                for n in range(4):
                    if A:
                        qk_high(n, i)
                    if Bs and n < 2:
                        exps(6 + n, b)
                    if n == 3 and more:
                        inv_std(0, following(i))
                if Bs:
                    inv_sum(0, b)

            pipeline(act, body)

        @block.vector
        def _(dve):
            def stats(k, src, pair, tiles):
                for t in tiles:
                    last = dve.bn_stats(bst[:, t, :], src[:, t, :])
                if t < T - 1:
                    return
                last.then_inc(ln_bst[k], 1)
                dve.wait_ge(ln_bst[k], count(pair))
                dve.wait_ge(ln_xn[1 - k], count(pair if k else prev(pair)))
                hold(dve, pair)
                for t in range(T):
                    last = dve.bn_aggr(mv[:, t, :], bst[:, t, :])
                last.then_inc(ln_mv[k], 1)

            dve.wait_ge(x_in, 16)
            stats(0, X, (None, 0), range(T))
            dve.wait_ge(a_in, 48)
            for j in range(2):
                for f in range(FT):
                    dve.tensor_tensor_reduce(out=C[:, j, f * F:(f + 1) * F], in0=WH[:, f, 0:F], in1=E0[:, 2 + j, :], scale=1.0, scalar=0.0,
                                             op0=ALU.mult, op1=ALU.add, accum_out=WH[:, f, F + j:F + j + 1]).then_inc(wa_made, 1)
            dve.tensor_scalar(nbg[:, :], nmr[:, 0:2], -1.0, None, ALU.mult).then_inc(bg_neg, 1)
            for n, (ps, hi, lo) in enumerate(((S0, wqh, wql), (S1, wkh, wkl), (T0, wvh, wvl))):
                dve.wait_ge(w_hi, n + 1)
                dve.tensor_tensor(lo[:, :, :].rearrange("p f o -> p (f o)"), ps[:, :],
                                  hi[:, :, :].rearrange("p f o -> p (f o)").bitcast(f32), ALU.subtract).then_inc(w_lo, 1)
            for n, ps in enumerate((BC, BR)):
                dve.wait_ge(w_hi, 4 + n)
                dve.tensor_tensor(wgl[:, 2 * n:2 * n + 2, :].rearrange("p f o -> p (f o)"), ps[:, :],
                                  wgh[:, 2 * n:2 * n + 2, :].rearrange("p f o -> p (f o)").bitcast(f32), ALU.subtract).then_inc(w_lo, 1)
            dve.wait_ge(w_hi, 6)
            dve.wait_ge(wa_made, 4)
            dve.tensor_tensor(w0l[:, :, :], WH[:, 0:2, :], w0h[:, :, :].bitcast(f32), ALU.subtract).then_inc(w_lo, 1)
            dve.wait_ge(bg_neg, 1)

            def relu_lo(layer, pair, dst, hi):
                for f in range(FT):
                    dve.wait_ge(h_hi[2 * layer + f], count(pair))
                    dve.scalar_tensor_tensor(out=dst[:, f, :], in0=(G0, G1)[f][:, :], scalar=0.0, in1=hi[:, f, :].bitcast(f32),
                                             op0=ALU.max, op1=ALU.subtract).then_inc(h_lo[2 * layer + f], 1)

            def qk_low(n, pair):
                dve.wait_ge(qk_hi, count(pair, n + 1, 4))
                dve.tensor_tensor(PR[n // 2][1][:, n % 2, :].bitcast(f32r), (G0, G1)[n % 2][:, :],
                                  PR[n // 2][0][:, n % 2, :], ALU.subtract).then_inc(qk_lo, 1)

            def score_max(u, pair, par):
                a, h = u // NH, HEADS[u % NH]
                dve.wait_ge(s_mm[u % 4], of_unit(pair, u))
                if u == 0:
                    dve.wait_ge(m_t, count(prev(pair), 2, 2))
                hold(dve, pair)
                for t in range(2):
                    ps = SB[u % 2][:, t * N:(t + 1) * N]
                    last = dve.tensor_tensor_reduce(out=ps, in0=ps, in1=MN[par][:, 2 * a + t, :],
                                                    scale=-1.0, scalar=BIG, op0=ALU.add, op1=ALU.min,
                                                    accum_out=NM[:, 2 * a + t, h:h + 1])
                last.then_inc(s_max[u % 4], 1)

            def max_parts(a, pair, ps):
                dve.wait_ge(m_t, count(pair, a + 1, 2))
                dve.wait_ge(max_in[1 - a], count(pair if a else prev(pair), 32, 32))
                dve.tensor_copy(MH[:, :], ps[0:NH, 0:N]).then_inc(m_hi, 1)
                dve.wait_ge(m_hi, count(pair, a + 1, 2))
                dve.tensor_tensor(ML[:, :], ps[0:NH, 0:N], MH[:, :].bitcast(f32), ALU.subtract).then_inc(m_lo, 1)

            def attention_out(a, pair):
                dve.wait_ge(r_inv, count(pair, a + 1, 2))
                if a == 0:
                    dve.wait_ge(z_mm, count(prev(pair), 2, 2))
                    dve.wait_ge(r_made, count(prev(pair), 2, 2))
                    dve.wait_ge(c_lo, count(prev(pair), 2, 2))
                dve.tensor_tensor(C[:, :, a * N:(a + 1) * N], BC[:, :].rearrange("p (f n) -> p f n", f=FT), RI[:, :, :],
                                  ALU.mult).then_inc(c_out, 1)

            def gate_cut(o, pair):
                dve.wait_ge(z_exp, count(pair, o + 1, 2))
                dve.tensor_scalar(G[:, o, :], G[:, o, :], EMAX, 1.0, ALU.min, ALU.add).then_inc(g_cut, 1)

            def mix_sum(o, pair):
                dve.wait_ge(gd_made, count(pair, o + 1, 2))
                dve.tensor_tensor(D[:, o, :], D[:, o, :], C[:, o, :], ALU.add).then_inc(r_made, 1)

            def output(h, pair, par):
                dve.wait_ge(r_t, count(pair, h + 1, 2))
                if h == 0:
                    dve.wait_ge(out_done, count(prev(pair), 32, 32))
                dve.tensor_tensor(OUT[:, 2 * h:2 * h + 2, :].rearrange("p t f -> p (t f)"), (G0, G1)[h][:, :],
                                  X1[par][:, 2 * h:2 * h + 2, :].rearrange("p t f -> p (t f)"), ALU.add).then_inc(fin, 1)

            def residual(h, pair):
                dve.wait_ge(hp_relu, count(pair, h + 1, 2))
                at = X[:, 2 * h:2 * h + 2, :].rearrange("p t f -> p (t f)")
                dve.scalar_tensor_tensor(out=at, in0=(G0, G1)[h][:, :], scalar=SLOPE, in1=at,
                                         op0=ALU.mult, op1=ALU.add).then_inc(hp_x, 1)

            def column_inverse(a, pair):
                dve.wait_ge(e0_exp, count(pair, a + 1, 2))
                dve.reciprocal(ri0[:, 2 * a:2 * a + 2], rs0[:, 2 * a:2 * a + 2]).then_inc(e0_rinv, 1)

            def body(i, par, A, Bs, Cs, more):
                b, c = prev(i), prev(i, 2)
                bp = 1 - par
                if A:
                    dve.wait_ge(adj_in, count(i, 16, 16))
                    dve.wait_ge(adj_t, count(b))
                    dve.tensor_scalar(CL[:, :, :], ADJ[:, :, :], 1.0, -1.0, ALU.min, ALU.max).then_inc(adj_cut, 1)
                    for u in range(UN - 4, UN):
                        dve.wait_ge(s_max[u % 4], of_unit(c, u))
                    dve.tensor_scalar(MN[par][:, :, :], ADJ[:, :, :], 0.0, NEG, ALU.is_equal, ALU.mult).then_inc(mn_made, 1)
                    relu_lo(0, i, HTl, HTh)
                    dve.wait_ge(clt_made, count(i))
                    for g in range(HG):
                        dve.wait_ge(stacked[0][g], count(b, 48, 48))
                    dve.tensor_scalar(E0[:, :, :], CLT[:, :, :], 0.0, NEG, ALU.is_le, ALU.mult).then_inc(m0_made, 1)
                if Bs:
                    dve.wait_ge(mn_made, count(b))
                    for u in range(5):
                        score_max(u, b, bp)
                if Cs:
                    attention_out(1, c)
                if A:
                    dve.wait_ge(sib_t, count(i))
                    dve.wait_ge(e0_add, count(i, 4, 4))
                    hold(dve, i)
                    for t in range(T):
                        a = t // 2
                        last = dve.tensor_tensor_reduce(out=E0[:, t, :], in0=G1[:, a * N:(a + 1) * N], in1=E0[:, t, :], scale=1.0,
                                                        scalar=-BIG, op0=ALU.add, op1=ALU.max, accum_out=mx0[:, t:t + 1])
                    last.then_inc(e0_max, 1)
                    dve.wait_ge(e0_max, count(i))
                    dve.tensor_scalar(nm0[:, :], mx0[:, :], -1.0, None, ALU.mult).then_inc(e0_nm, 1)
                    dve.wait_ge(e0_nm, count(i))
                    dve.scalar_tensor_tensor(out=ngm[:, :], in0=nm0[:, :], scalar=SLOPE, in1=nm0[:, :], op0=ALU.mult,
                                             op1=ALU.min).then_inc(e0_ngm, 1)
                    dve.wait_ge(e0_ngm, count(i))
                    for a in range(2):
                        e0 = E0[:, 2 * a:2 * a + 2, :].rearrange("p t n -> p (t n)")
                        dve.scalar_tensor_tensor(out=e0, in0=e0, scalar=SLOPE, in1=e0, op0=ALU.mult, op1=ALU.max).then_inc(e0_leaky, 1)
                if Bs:
                    score_max(5, b, bp)
                if A:
                    column_inverse(0, i)
                if Bs:
                    score_max(6, b, bp)
                if A:
                    column_inverse(1, i)
                if Bs:
                    score_max(7, b, bp)
                if Cs:
                    gate_cut(0, c)
                if Bs:
                    max_parts(0, b, S0)
                if Cs:
                    gate_cut(1, c)
                if A:
                    residual(0, i)
                    residual(1, i)
                    dve.wait_ge(x1_made, count(i, 1, 2))
                    stats(1, X, i, (0, 1))
                if Bs:
                    score_max(NH, b, bp)
                if A:
                    dve.wait_ge(x1_made, count(i, 2, 2))
                    stats(1, X, i, (2, 3))
                if Cs:
                    mix_sum(0, c)
                if A:
                    dve.wait_ge(ln_rstd[1], count(i))
                    dve.scalar_tensor_tensor(out=nmr[:, :], in0=mv[:, :, 0], scalar=-1.0, in1=rstd[:, :], op0=ALU.mult,
                                             op1=ALU.mult).then_inc(ln_nmr, 1)
                if Cs:
                    mix_sum(1, c)
                if Bs:
                    score_max(NH + 1, b, bp)
                if Cs:
                    output(0, c, par)
                    output(1, c, par)
                if Bs:
                    score_max(NH + 2, b, bp)
                if A:
                    relu_lo(1, i, H2l[par], H2h[par])
                if Bs:
                    score_max(NH + 3, b, bp)
                if A:
                    dve.wait_ge(fin, count(c, 2, 2))
                    dve.tensor_copy(X1[par][:, :, :], X[:, :, :]).then_inc(x1_kept, 1)
                if Bs:
                    score_max(NH + 4, b, bp)
                if A:
                    qk_low(0, i)
                if Bs:
                    score_max(NH + 5, b, bp)
                    score_max(NH + 6, b, bp)
                if A:
                    qk_low(1, i)
                if more:
                    dve.wait_ge(x_in, count(following(i), 16, 16))
                    stats(0, X, following(i), (0, 1))
                if Bs:
                    score_max(NH + 7, b, bp)
                if more:
                    stats(0, X, following(i), (2, 3))
                if A:
                    qk_low(2, i)
                if Bs:
                    max_parts(1, b, S0)
                if A:
                    qk_low(3, i)
                    dve.tensor_scalar(M1[par][:, :, :], CLT[:, :, :], 0.0, NEG, ALU.is_equal, ALU.mult).then_inc(m1_made, 1)
                if Bs:
                    attention_out(0, b)

            pipeline(dve, body)

        @block.tensor
        def _(pe):
            pe.wait_ge(c_made, 6)
            srcs = ((0, S0, D[:, 0, :].rearrange("p (f c) -> p f c", f=FT)), (1, S1, D[:, 1, :].rearrange("p (f c) -> p f c", f=FT)),
                    (2, T0, E0[:, 0:2, :]), (3, BC, G[:, :, 0:F]), (3, BR, G[:, :, F:2 * F]))
            for n, ps, src in srcs:
                pe.wait_ge(w_in[n], 16)
                for f in range(FT):
                    for o in range(FT):
                        last = pe.transpose(ps[:, f * F + o * P:f * F + (o + 1) * P], src[:, o, f * P:(f + 1) * P], ident[:, :])
                last.then_inc(w_tr, 1)
            pe.wait_ge(w_lo, 6)
            pe.wait_ge(ks_ones, 2)

            def split(ps, tiles, first, end, only=None):
                for n, terms in enumerate((((0, 2), (1, 2)), ((0, 3),))):
                    if only is None or only == n:
                        for k, tile in enumerate(tiles):
                            for m, (l, r) in enumerate(terms):
                                last = pe.matmul(ps, tile[l], tile[r], start=first and n + k + m == 0,
                                                 stop=end and n == 1 and k == len(tiles) - 1)
                return last

            def feature_transposes(layer, f, ps):
                for t in range(T):
                    last = pe.transpose(ps[:, t * P:(t + 1) * P], XN[:, t, f * P:(f + 1) * P], ident[:, :])
                last.then_inc(h_t[2 * layer + f], 1)

            def scores(u, pair, par):
                a, h = u // NH, HEADS[u % NH]
                if u < NH and u % 2 == 0:
                    pe.wait_ge(stacked[0][h % HG], count(pair, 48, 48))
                    pe.wait_ge(stacked[1][h % HG], count(pair, 48, 48))
                if u % NH == 0:
                    pe.wait_ge(m_lo, count(pair if u else prev(pair), 1 if u else 2, 2))
                if u >= 2:
                    pe.wait_ge(s_max[(u - 2) % 4], of_unit(pair, u - 2))
                else:
                    pe.wait_ge(s_max[(UN + u - 2) % 4], of_unit(prev(pair), UN + u - 2))
                for t in range(2):
                    last = pe.matmul(SB[u % 2][:, t * N:(t + 1) * N], QS[par][0:KR, h, a * N + t * P:a * N + (t + 1) * P],
                                     KS[par][0:KR, h, a * N:(a + 1) * N], start=True, stop=True)
                last.then_inc(s_mm[u % 4], 1)

            def scores_t(u, pair, par):
                a, h = u // NH, u % NH
                if h == 0:
                    pe.wait_ge(max_in[a], count(pair, 32, 32))
                    pe.wait_ge(m1_made, count(pair))
                if u >= 2:
                    pe.wait_ge(p_exp[(u - 2) % 4], of_unit(pair, u - 2))
                else:
                    pe.wait_ge(p_exp[(UN + u - 2) % 4], of_unit(prev(pair), UN + u - 2))
                ps = TB[u % 2]
                pe.matmul(ps[:, :], identb[:, :], M1[par][:, 2 * a:2 * a + 2, :].rearrange("p t n -> p (t n)"),
                          start=True, stop=False)
                for t in range(2):
                    last = pe.matmul(ps[:, t * N:(t + 1) * N], KS[par][0:KM, h, a * N + t * P:a * N + (t + 1) * P],
                                     QS[par][0:KM, h, a * N:(a + 1) * N], start=False, stop=(t == 1))
                last.then_inc(st_mm[u % 4], 1)

            def weighted(g, pair, par):
                a, o = g // 2, g % 2
                if o == 0:
                    if a == 0:
                        pe.wait_ge(z_exp, count(prev(pair), 2, 2))
                    else:
                        pe.wait_ge(c_out, count(pair, 1, 2))
                for rhs_ones in (False, True):
                    ps = BR if rhs_ones else BC
                    for t in range(2):
                        for k in range(HG):
                            u = 4 * g + k
                            if t == 0 and not rhs_ones:
                                pe.wait_ge(p_exp[u % 4], of_unit(pair, u))
                            lhs = ones[:, :] if rhs_ones else V[par][:, 2 * a + t, o * P + k * DK:o * P + (k + 1) * DK]
                            last = pe.matmul(ps[k * DK:(k + 1) * DK, o * N:(o + 1) * N], lhs, PT[u % PTS][:, t * N:(t + 1) * N],
                                             start=(t == 0), stop=(t == 1))
                last.then_inc(pv_mm, 1)

            def max_transposes(a, pair):
                for u in range(NH * a + 4, NH * a + NH):
                    pe.wait_ge(s_max[u % 4], of_unit(pair, u))
                for t in range(2):
                    last = pe.transpose(S0[0:NH, t * P:(t + 1) * P], NM[:, 2 * a + t, :], ident[:, :])
                last.then_inc(m_t, 1)

            def gate(o, half, par, only=None):
                hi, lo = (H2h[par], H2l[par]) if half == "x" else (Ch, Cl)
                k = FT if half == "x" else 0
                return split((BC, BR)[o][:, :], [(wgh[:, f + k, o * P:(o + 1) * P], wgl[:, f + k, o * P:(o + 1) * P],
                                                  hi[:, f, :], lo[:, f, :]) for f in range(FT)],
                             half == "x", half == "c", only=only)

            def products(t, pair):
                s = slice(t * P, (t + 1) * P)
                split((G1, G0)[t % 2][:, 0:F + 2], [(HTh[:, f, s], HTl[:, f, s], w0h[:, f, :], w0l[:, f, :]) for f in range(FT)],
                      True, True).then_inc(wh_mm, 1)

            def values(n, pair, par):
                pe.wait_ge(qk_lo, count(pair, n + 3, 4))
                for t in (2 * n, 2 * n + 1):
                    s = slice(t * P, (t + 1) * P)
                    last = split((G0, G1)[n][:, (t % 2) * F:(t % 2 + 1) * F],
                                 [(H2h[par][:, f, s], H2l[par][:, f, s], wvh[:, f, :], wvl[:, f, :]) for f in range(FT)], True, True)
                last.then_inc(v_mm, 1)

            def qk_product(n, pair, par):
                ps, o = (G0, G1)[n % 2], n % 2
                if n < 2:
                    pe.wait_ge(h_lo[2 + n], count(pair))
                else:
                    pe.wait_ge(qk_lo, count(pair, n - 1, 4))
                wh_, wl_ = ((wqh, wql), (wkh, wkl))[n // 2]
                tiles = [(wh_[:, f, o * P:(o + 1) * P], wl_[:, f, o * P:(o + 1) * P], H2h[par][:, f, :], H2l[par][:, f, :])
                         for f in range(FT)]
                split(ps[:, :], tiles, True, True, only=0)
                if n == 0:
                    pe.wait_ge(h_lo[3], count(pair))
                split(ps[:, :], tiles, True, True, only=1).then_inc(qk_mm, 1)

            def graph_sum(a, pair):
                pe.wait_ge(wh_norm, count(pair, a + 1, 2))
                for t in range(2):
                    for j in range(2):
                        last = pe.matmul((G0, G1)[a][:, t * F:(t + 1) * F], E0[:, 2 * a + j, t * P:(t + 1) * P],
                                         WH[:, 2 * a + j, 0:F], start=(j == 0), stop=(j == 1))
                last.then_inc(hp_mm, 1)

            def result_transposes(h):
                for t in (2 * h, 2 * h + 1):
                    for f in range(FT):
                        last = pe.transpose((G0, G1)[h][:, (t % 2) * F + f * P:(t % 2) * F + (f + 1) * P],
                                            D[:, f, t * P:(t + 1) * P], ident[:, :])
                last.then_inc(r_t, 1)

            def body(i, par, A, Bs, Cs, more):
                b, c = prev(i), prev(i, 2)
                bp = 1 - par
                if Bs:
                    values(0, b, bp)
                    values(1, b, bp)
                for n in range(8):
                    if Cs:
                        scores_t(NH + n, c, par)
                    if A and n in (1, 2):
                        if n == 1:
                            pe.wait_ge(ln_xn[0], count(i))
                        pe.wait_ge(v_out, count(b, n, 2))
                        feature_transposes(0, n - 1, (G0, G1)[n - 1])
                    if Cs and n == 4:
                        weighted(2, c, par)
                    if A and n == 4:
                        pe.wait_ge(adj_cut, count(i))
                        pe.wait_ge(h_lo[0], count(i))
                        for t in range(T):
                            for j in range(2):
                                at = ((t // 2) * 2 + j) * N + (t % 2) * P
                                last = pe.transpose(G0[:, :].bitcast(bf16)[:, at:at + P], CL[:, t, j * P:(j + 1) * P], identb[:, :])
                        last.then_inc(adj_t, 1)
                    if A and n > 4:
                        t = n - 5
                        if t == 0:
                            pe.wait_ge(h_lo[1], count(i))
                        elif t == 1:
                            pe.wait_ge(clt_made, count(i))
                        else:
                            pe.wait_ge(wh_out, count(i, t - 1, 4))
                        products(t, i)
                    if Bs and n > 4:
                        scores(n - 5, b, bp)
                if Bs:
                    scores(3, b, bp)
                if Cs:
                    weighted(3, c, par)
                if Bs:
                    scores(4, b, bp)
                if A:
                    pe.wait_ge(wh_out, count(i, 2, 4))
                    products(3, i)
                if Bs:
                    scores(5, b, bp)
                if A:
                    for t in range(T):
                        pe.wait_ge(wh_out, count(i, max(t + 1, 3), 4))
                        last = pe.transpose(G1[:, t * P:(t + 1) * P], WH[:, t, F:F + 1].broadcast_to([P, P]), ident[:, :])
                    last.then_inc(sib_t, 1)
                if Cs:
                    pe.wait_ge(c_out, count(c, 2, 2))
                    gate(0, "x", par)
                    gate(1, "x", par)
                if Bs:
                    scores(6, b, bp)
                if Cs:
                    pe.wait_ge(c_hi, count(c, 2, 2))
                    gate(0, "c", par, only=0)
                    pe.wait_ge(c_lo, count(c, 2, 2))
                    gate(0, "c", par, only=1).then_inc(z_mm, 1)
                if Bs:
                    scores(7, b, bp)
                if Cs:
                    gate(1, "c", par).then_inc(z_mm, 1)
                if Bs:
                    max_transposes(0, b)
                if A:
                    graph_sum(0, i)
                if A:
                    pe.wait_ge(e0_max, count(i))
                    graph_sum(1, i)
                if Bs:
                    scores(NH, b, bp)
                    scores(NH + 1, b, bp)
                    scores_t(0, b, bp)
                    scores_t(1, b, bp)
                    scores_t(2, b, bp)
                    scores_t(3, b, bp)
                    scores_t(4, b, bp)
                    pe.wait_ge(v_out, count(b, 2, 2))
                    weighted(0, b, bp)
                    scores(NH + 2, b, bp)
                if Cs:
                    pe.wait_ge(r_made, count(c, 2, 2))
                    for h in range(2):
                        if A:
                            pe.wait_ge(hp_x, count(i, h + 1, 2))
                        result_transposes(h)
                if Bs:
                    scores(NH + 3, b, bp)
                if A:
                    pe.wait_ge(ln_xn[1], count(i))
                    for f in range(FT):
                        pe.wait_ge(hp_x, count(i, f + 1, 2))
                        pe.wait_ge(fin, count(c, f + 1, 2))
                        feature_transposes(1, f, (G0, G1)[f])
                if Bs:
                    scores(NH + 4, b, bp)
                    scores_t(5, b, bp)
                for n in range(4):
                    if A and n == 0:
                        pe.wait_ge(h_hi[2], count(i))
                        pe.wait_ge(h_hi[3], count(i))
                    if A:
                        qk_product(n, i, par)
                    if Bs:
                        if n == 0:
                            scores(NH + 5, b, bp)
                            scores_t(6, b, bp)
                        elif n == 1:
                            scores(NH + 6, b, bp)
                            scores_t(7, b, bp)
                            scores(NH + 7, b, bp)
                        elif n == 3:
                            max_transposes(1, b)
                            weighted(1, b, bp)

            pipeline(pe, body)


_INS = ["x", "adj", "L0_gnn_W", "L0_gnn_a", "L1_gnn_Wq", "L1_gnn_Wk", "L1_gnn_Wv", "L1_gnn_Wg", "L1_gnn_bg"]


def kernel(**inputs):
    import numpy as _np
    import concourse.bacc as _bacc
    from concourse import mybir as _mybir
    from concourse.bass_utils import run_bass_kernel_spmd as _run

    nc = _bacc.Bacc("TRN2", target_bir_lowering=False, num_devices=1)
    arrays, args = {}, []
    for name in _INS:
        a = _np.ascontiguousarray(inputs[name])
        arrays[f"in_{name}"] = a
        args.append(nc.dram_tensor(f"in_{name}", a.shape, _mybir.dt.from_np(a.dtype), kind="ExternalInput").ap())
    shape = inputs["x"].shape
    args.append(nc.dram_tensor("out_dram", shape, _mybir.dt.from_np(_np.dtype("float32")), kind="ExternalOutput").ap())
    gnn_kernel(nc, *args)
    r = _run(nc, [arrays], core_ids=[0])
    return r.results[0]["out_dram"]
```
